# Optimizing a Trainium2 kernel written in Bass

```python
import numpy as np
import jax
import jax.numpy as jnp

def _softmax(x, axis=-1):
    return jax.nn.softmax(x, axis=axis)

def _gelu(x):
    return jax.nn.gelu(x, approximate=True)

def _silu(x):
    return jax.nn.silu(x)

def _sigmoid(x):
    return jax.nn.sigmoid(x)

def _layernorm(x, axis=-1, eps=1e-05):
    m = jnp.mean(x, axis=axis, keepdims=True)
    v = jnp.var(x, axis=axis, keepdims=True)
    return (x - m) / jnp.sqrt(v + eps)

def _scatter_add(tgt, idx, src, axis=0):
    return tgt.at[idx].add(src)

def _segment_sum(src, seg, n):
    return jax.ops.segment_sum(src, seg, n)
kernel_name = 'mk_gnn_preln_d2_gnn_r32_837105'

def setup_inputs(seed: int=0):
    np.random.seed(seed)
    _w = jnp.asarray

    def _rec_inputs():
        import jax
        import jax.numpy as jnp
        _gk = jax.random.key(seed)
        x = -0.000364 + 1 * jax.random.normal(jax.random.fold_in(_gk, 1), (30000, 512), jnp.float32)
        src = jax.random.randint(jax.random.fold_in(_gk, 2), (30000,), 0, 30000, jnp.int32)
        dst = jax.random.randint(jax.random.fold_in(_gk, 3), (30000,), 0, 30000, jnp.int32)
        _o = jnp.argsort(dst, stable=True)
        src = src[_o]
        dst = dst[_o]
        return (x, src, dst)
    x, src, dst = _rec_inputs()

    def _L0_gnn_setup():
        import jax, jax.numpy as jnp
        import numpy as np
        N = 30000
        E = 15000
        D_IN = 512
        D_HID = 512
        D_OUT = 512
        EPS = 1e-05

        def gcn_conv(x, W, b, src, dst, n_nodes):
            xw = x @ W
            loop = jnp.arange(n_nodes, dtype=src.dtype)
            s = jnp.concatenate([src, loop])
            d = jnp.concatenate([dst, loop])
            deg = jax.ops.segment_sum(jnp.ones_like(d, dtype=xw.dtype), d, num_segments=n_nodes)
            dinv = jnp.where(deg > 0, jax.lax.rsqrt(deg), 0.0)
            norm = dinv[s] * dinv[d]
            msg = norm[:, None] * xw[s]
            out = jax.ops.segment_sum(msg, d, num_segments=n_nodes)
            return out + b

        def layer_norm(x, gamma, beta):
            mu = jnp.mean(x, axis=-1, keepdims=True)
            var = jnp.mean(jnp.square(x - mu), axis=-1, keepdims=True)
            return (x - mu) * jax.lax.rsqrt(var + EPS) * gamma + beta
        key = jax.random.key(seed)
        ks = jax.random.split(key, 8)
        x = jax.random.normal(ks[0], (N, D_IN), dtype=jnp.float32)
        edge_index = jax.random.randint(ks[1], (2, E), 0, N, dtype=jnp.int64)
        batch = jnp.zeros((N,), dtype=jnp.int64)
        s1 = 1.0 / np.sqrt(D_IN)
        s2 = 1.0 / np.sqrt(D_HID)
        W1 = jax.random.uniform(ks[2], (D_IN, D_HID), jnp.float32, -s1, s1)
        b1 = jnp.zeros((D_HID,), jnp.float32)
        W2 = jax.random.uniform(ks[3], (D_HID, D_OUT), jnp.float32, -s2, s2)
        b2 = jnp.zeros((D_OUT,), jnp.float32)
        gamma1 = jnp.ones((D_HID,), jnp.float32)
        beta1 = jnp.zeros((D_HID,), jnp.float32)
        gamma2 = jnp.ones((D_OUT,), jnp.float32)
        beta2 = jnp.zeros((D_OUT,), jnp.float32)
        return {'x': x, 'edge_index': edge_index, 'batch': batch, 'W1': W1, 'b1': b1, 'gamma1': gamma1, 'beta1': beta1, 'W2': W2, 'b2': b2, 'gamma2': gamma2, 'beta2': beta2}
    _L0_gnn_all = _L0_gnn_setup()
    _L0_gnn_in = {k: v for k, v in _L0_gnn_all.items() if k in ('W1', 'b1', 'gamma1', 'beta1', 'W2', 'b2', 'gamma2', 'beta2')}
    del _L0_gnn_all

    def _L1_gnn_setup():
        import jax, jax.numpy as jnp
        import numpy as np
        key = jax.random.key(seed)
        k1, k2, k3 = jax.random.split(key, 3)
        N, E, D = (10000, 5000, 512)
        x = jax.random.normal(k1, (N, D), dtype=jnp.float32)
        edge_index = jax.random.randint(k2, (2, E), 0, N, dtype=jnp.int64)
        W = jax.random.normal(k3, (D, D), dtype=jnp.float32) * (1.0 / np.sqrt(D))
        b = jnp.zeros((D,), dtype=jnp.float32)
        return {'x': x, 'edge_index': edge_index, 'W': W, 'b': b}
    _L1_gnn_all = _L1_gnn_setup()
    _L1_gnn_in = {k: v for k, v in _L1_gnn_all.items() if k in ('W', 'b')}
    del _L1_gnn_all
    return {'x': x, 'src': src, 'dst': dst, 'L0_gnn_W1': _L0_gnn_in['W1'], 'L0_gnn_b1': _L0_gnn_in['b1'], 'L0_gnn_gamma1': _L0_gnn_in['gamma1'], 'L0_gnn_beta1': _L0_gnn_in['beta1'], 'L0_gnn_W2': _L0_gnn_in['W2'], 'L0_gnn_b2': _L0_gnn_in['b2'], 'L0_gnn_gamma2': _L0_gnn_in['gamma2'], 'L0_gnn_beta2': _L0_gnn_in['beta2'], 'L1_gnn_W': _L1_gnn_in['W'], 'L1_gnn_b': _L1_gnn_in['b']}

def reference(x, src, dst, L0_gnn_W1, L0_gnn_b1, L0_gnn_gamma1, L0_gnn_beta1, L0_gnn_W2, L0_gnn_b2, L0_gnn_gamma2, L0_gnn_beta2, L1_gnn_W, L1_gnn_b):
    import jax
    import jax.numpy as jnp

    def _L0_gnn_ref(x, edge_index, batch, W1, b1, gamma1, beta1, W2, b2, gamma2, beta2):
        import jax, jax.numpy as jnp
        import numpy as np
        N = 30000
        E = 15000
        D_IN = 512
        D_HID = 512
        D_OUT = 512
        EPS = 1e-05

        def gcn_conv(x, W, b, src, dst, n_nodes):
            xw = x @ W
            loop = jnp.arange(n_nodes, dtype=src.dtype)
            s = jnp.concatenate([src, loop])
            d = jnp.concatenate([dst, loop])
            deg = jax.ops.segment_sum(jnp.ones_like(d, dtype=xw.dtype), d, num_segments=n_nodes)
            dinv = jnp.where(deg > 0, jax.lax.rsqrt(deg), 0.0)
            norm = dinv[s] * dinv[d]
            msg = norm[:, None] * xw[s]
            out = jax.ops.segment_sum(msg, d, num_segments=n_nodes)
            return out + b

        def layer_norm(x, gamma, beta):
            mu = jnp.mean(x, axis=-1, keepdims=True)
            var = jnp.mean(jnp.square(x - mu), axis=-1, keepdims=True)
            return (x - mu) * jax.lax.rsqrt(var + EPS) * gamma + beta
        src, dst = (edge_index[0], edge_index[1])
        residual = x
        h = gcn_conv(x, W1, b1, src, dst, N)
        h = layer_norm(h, gamma1, beta1)
        h = jax.nn.gelu(h, approximate=False)
        h = gcn_conv(h, W2, b2, src, dst, N)
        h = layer_norm(h, gamma2, beta2)
        return jax.nn.gelu(h + residual, approximate=False)

    def _L1_gnn_ref(x, edge_index, W, b):
        import jax, jax.numpy as jnp
        import numpy as np
        N = x.shape[0]
        loop = jnp.arange(N, dtype=edge_index.dtype)
        src = jnp.concatenate([edge_index[0], loop])
        dst = jnp.concatenate([edge_index[1], loop])
        deg = jax.ops.segment_sum(jnp.ones(src.shape, dtype=x.dtype), dst, num_segments=N)
        deg_inv_sqrt = jnp.where(deg > 0, jax.lax.rsqrt(deg), 0.0)
        norm = deg_inv_sqrt[src] * deg_inv_sqrt[dst]
        h = x @ W
        msg = h[src] * norm[:, None]
        out = jax.ops.segment_sum(msg, dst, num_segments=N) + b
        return out
    edge_index = jnp.stack([src, dst])
    batch0 = jnp.zeros((30000,), jnp.int32)
    h = jnp.maximum(_layernorm(x, axis=-1), 0.0)
    x = x + _L0_gnn_ref(h, edge_index, batch0, L0_gnn_W1, L0_gnn_b1, L0_gnn_gamma1, L0_gnn_beta1, L0_gnn_W2, L0_gnn_b2, L0_gnn_gamma2, L0_gnn_beta2)
    h = jnp.maximum(_layernorm(x, axis=-1), 0.0)
    x = x + _L1_gnn_ref(h, edge_index, L1_gnn_W, L1_gnn_b)
    return x

_drawn_inputs = setup_inputs


def setup_inputs(seed=0):
    import zlib

    import numpy as np

    out = dict(_drawn_inputs(seed))
    spreads = {'L0_gnn_b1': (0.0, 0.1),
     'L0_gnn_gamma1': (1.0, 0.2),
     'L0_gnn_beta1': (0.0, 0.1),
     'L0_gnn_b2': (0.0, 0.1),
     'L0_gnn_gamma2': (1.0, 0.2),
     'L0_gnn_beta2': (0.0, 0.1),
     'L1_gnn_b': (0.0, 0.1)}
    factors = {}
    for name, (base, spread) in spreads.items():
        noise = np.random.default_rng([zlib.crc32(name.encode()), seed]).standard_normal(out[name].shape)
        drawn = base * np.exp(spread * noise) if base else spread * noise
        out[name] = jnp.asarray(drawn.astype(out[name].dtype))
    for name, factor in factors.items():
        out[name] = (out[name] * factor).astype(out[name].dtype)
    return out
```

```python
from contextlib import ExitStack

import concourse.bass as bass
from concourse import mybir

P = 128
ALU = mybir.AluOpType
ACT = mybir.ActivationFunctionType
F32 = mybir.dt.float32
F32R = mybir.dt.float32r
BF16 = mybir.dt.bfloat16
I32 = mybir.dt.int32

EPS = 1e-5
SLOTS = 3
NORM_SLOTS = 6
CHUNKS = 2
WINDOW = CHUNKS * P
NOWHERE = 1 << 16


class Tile:

    def __init__(self, i, u, slots):
        self.i, self.u, self.slots = i, u, slots

    @property
    def n(self):
        return self.i * self.slots + self.u

    def after(self, k):
        return Tile(self.i + (self.u + k) // self.slots, (self.u + k) % self.slots, self.slots)


def run_tiles(engine, count, slots, body):
    rounds = (count - 1) // slots
    last = rounds - 1 if rounds > 2 else 1
    for n in range(slots):
        body(Tile(0, n, slots), n)
    if last > 1:
        with engine.Fori(1, last) as i:
            for u in range(slots):
                body(Tile(i, u, slots), None)
    for n in range(last * slots, count):
        body(Tile(n // slots, n % slots, slots), n)


def gnn_kernel(nc, x, src, dst, W1, b1, g1, be1, W2, b2, g2, be2, W3, b3, out, force_general=False):
    N, D = x.shape
    E = src.shape[0]
    NT = -(-N // P)
    NP = NT * P
    LAST = N - (NT - 1) * P
    NC = -(-E // P)
    EL = E - (NC - 1) * P
    KD = D // P
    THALF = [(h, min(P, NT - h * P)) for h in range(-(-NT // P))]
    CHALF = [(h, min(P, NC - h * P)) for h in range(-(-NC // P))]
    TRASH = NP + P
    ROWS = NP + 2 * P
    assert D == 512 and NT <= 2 * P and NC <= 2 * P and NT > 3 * SLOTS

    with ExitStack() as ctx:
        def sb(name, shape, dt=F32):
            return ctx.enter_context(nc.sbuf_tensor(name, shape, dt))

        def sem(name):
            return ctx.enter_context(nc.semaphore(name))

        def scratch(name, shape, dt=F32):
            return nc.dram_tensor(name, shape, dt, kind="Internal").ap()

        H = [scratch(f"H{q}", (2 * ROWS, D)) for q in range(3)]
        X2 = scratch("X2", (NP, D))
        SRC = scratch("src_padded", (E + 2 * WINDOW, 1), I32)
        DST = scratch("dst_padded", (E + 2 * WINDOW, 1), I32)

        ident = sb("ident", [P, P])
        ones = sb("ones", [P, P])
        before = sb("before", [P, P])
        after = sb("after", [P, P])
        col_i = sb("col_i", [P, 2 * P], I32)
        row_i = sb("row_i", [P, 1], I32)
        col = sb("col", [P, 2 * P])
        colb = sb("colb", [P, 2 * P], BF16)
        row = sb("row", [P, 2])
        neg_half = sb("neg_half", [P, 2 * P])
        dinv = sb("dinv", [P, NT])
        dinv2 = sb("dinv2", [P, NT])
        edge_to = sb("edge_to", [P, CHUNKS, NT])
        edge_from = sb("edge_from", [P, CHUNKS, NT], I32)
        rstd_x = sb("rstd_x", [P, NT])
        nb_x = sb("nb_x", [P, NT])
        general = sb("general", [P, 1], I32)
        Whi = [sb(f"Whi{q}", [P, KD, D], F32R) for q in range(3)]
        Wlo = [sb(f"Wlo{q}", [P, KD, D], F32R) for q in range(3)]
        vecs = [sb(f"vec{k}", [P, D]) for k in range(7)]
        bias_b, gamma_b, beta_b = vecs[0:3], vecs[3:5], vecs[5:7]

        Self = [sb(f"self{u}", [P, D]) for u in range(SLOTS)]
        G = [sb(f"g{u}", [P, CHUNKS, D]) for u in range(SLOTS)]
        S = [sb(f"s{u}", [P, CHUNKS, P]) for u in range(SLOTS)]
        Ahi = [sb(f"ahi{u}", [P, D], F32R) for u in range(SLOTS)]
        Alo = [sb(f"alo{u}", [P, D], F32R) for u in range(SLOTS)]
        Cv = [sb(f"conv{u}", [P, D]) for u in range(SLOTS)]
        Y = [sb(f"y{u}", [P, D]) for u in range(SLOTS)]
        Xt = [sb(f"x{u}", [P, D]) for u in range(SLOTS)]
        R = [sb(f"r{u}", [P, D]) for u in range(SLOTS)]
        X2t = [sb(f"x2{u}", [P, D]) for u in range(SLOTS)]
        Ho = [sb(f"ho{u}", [P, D]) for u in range(SLOTS)]
        small = [sb(f"small{u}", [P, 16]) for u in range(NORM_SLOTS)]
        small2 = [sb(f"smallb{u}", [P, 16]) for u in range(SLOTS)]
        idx = [sb(f"idx{u}", [P, CHUNKS], I32) for u in range(SLOTS)]

        bank = [ctx.enter_context(nc.psum_tensor(f"bank{b}", [P, 512], F32)) for b in range(8)]
        Agg, Out = bank[0:SLOTS], bank[SLOTS:2 * SLOTS]

        step = sem("prep_step")
        done = [0]

        def then(ins):
            done[0] += 1
            ins.then_inc(step, 1)
            return done[0]

        ints = sb("ints", [P, 2, WINDOW], I32)
        ints2 = sb("ints2", [P, 2, WINDOW], I32)
        fl = sb("fl", [P, 2, WINDOW])
        fl2 = sb("fl2", [P, 2, WINDOW])
        lo_t = sb("lo_t", [P, NC])
        hi_t = sb("hi_t", [P, NC])
        deg = sb("deg", [P, NT])
        oh_lo = [sb(f"oh_lo{u}", [P, P], BF16) for u in range(4)]
        oh_hi = [sb(f"oh_hi{u}", [P, 2 * P], BF16) for u in range(4)]
        cnt = sb("cnt", [P, 2])
        start_i = sb("start_i", [P, 2], I32)
        seen = sb("seen", [P, 2])
        ok = sb("ok", [P, 2])
        pad_i = sb("pad_i", [2, WINDOW], I32)

        loaded = sem("edges_loaded")
        weights = sem("weights_loaded")
        padded = sem("edges_padded")
        pads = sem("pads_written")
        consts = sem("consts_made")
        cols = sem("columns_made")
        dve1 = sem("dve_step")
        w_split = sem("weights_split")
        w_free = sem("weights_staged_free")
        turned = sem("edges_turned")
        hot_made = sem("one_hots_made")
        hot_used = sem("one_hots_used")
        counted = sem("degrees_counted")
        windows = sem("windows_fetched")

        stage = [Self[0], Self[1], Self[2], Xt[0]]

        with nc.Block() as block:
            @block.sync
            def _(sp):
                sp.wait_ge(consts, 1)
                for h, rows in CHALF:
                    full = rows if h < len(CHALF) - 1 or EL == P else rows - 1
                    sp.dma_start(ints[0:full, h, 0:P],
                                 dst[h * P * P:(h * P + full) * P].rearrange("(c j) -> c j", j=P)).then_inc(loaded, 16)
                    if full < rows:
                        sp.dma_start(ints[full:rows, h, 0:EL],
                                     dst[(NC - 1) * P:E].rearrange("(a j) -> a j", a=1)).then_inc(loaded, 16)
                for a, b in ((src, SRC), (dst, DST)):
                    r = next(k for k in (16, 15, 12, 10, 8, 6, 5, 4, 3, 2, 1) if E % k == 0)
                    sp.dma_start(b[0:E, :].rearrange("(a j) o -> a (j o)", a=r),
                                 a.rearrange("(a j) -> a j", a=r)).then_inc(padded, 16)
                sp.wait_ge(pads, 1)
                sp.dma_start(SRC[E:E + 2 * WINDOW, :].rearrange("(a j) o -> a (j o)", a=2), pad_i[:, :])\
                    .then_inc(padded, 16)
                sp.wait_ge(padded, 48)
                sp.wait_ge(pads, 2)
                sp.dma_start(DST[E:E + 2 * WINDOW, :].rearrange("(a j) o -> a (j o)", a=2), pad_i[:, :])\
                    .then_inc(padded, 16)
                for k, v in enumerate((b1, b2, b3, g1, g2, be1, be2)):
                    sp.dma_start(vecs[k][:, :], v.rearrange("(a d) -> a d", a=1).broadcast_to([P, D]))\
                        .then_inc(weights, 16)
                for q, w in enumerate((W1, W2, W3)):
                    wv = w.rearrange("(k p) n -> k p n", p=P)
                    if q:
                        sp.wait_ge(w_free, 4 * q)
                    for k in range(KD):
                        sp.dma_start(stage[k][:, :], wv[k, :, :]).then_inc(weights, 16)
                sp.wait_ge(weights, 16 * (7 + 3 * KD))
                sp.wait_ge(padded, 64)

            @block.gpsimd
            def _(pool):
                nc.gpsimd.memset(ints[:, :, :], -1).then_inc(consts, 1)
                nc.gpsimd.iota(col_i[:, :], pattern=[[1, 2 * P]], base=0, channel_multiplier=0).then_inc(cols, 1)
                nc.gpsimd.iota(row_i[:, :], pattern=[[0, 1]], base=0, channel_multiplier=1).then_inc(cols, 1)
                nc.gpsimd.memset(pad_i[:, :], 0).then_inc(pads, 1)
                pool.wait_ge(padded, 48)
                nc.gpsimd.memset(pad_i[:, :], NP).then_inc(pads, 1)
                pool.wait_ge(counted, 2)
                nc.gpsimd.tensor_tensor(dinv[:, :], dinv2[:, :], neg_half[:, 0:NT], ALU.pow).then_inc(counted, 1)
                pool.wait_ge(counted, 5)
                pool.wait_ge(padded, 64)
                for h, rows in THALF:
                    for a, o in ((SRC, ints2), (DST, ints)):
                        pool.indirect_dma_start(
                            o[0:rows, h, :], None, a,
                            bass.IndirectOffsetOnAxis(ap=start_i[0:rows, h:h + 1], axis=0),
                            bounds_check=E, oob_is_err=False).then_inc(windows, 16)

            @block.scalar
            def _(act):
                for q in range(3):
                    for k in range(KD):
                        act.wait_ge(weights, 16 * (7 + KD * (q + 1)))
                        nc.scalar.activation(Whi[q][:, k, :], stage[k][:, :], ACT.Copy).then_inc(w_split, 1)

            @block.vector
            def _(dve):
                n = [0]

                def link(ins):
                    n[0] += 1
                    ins.then_inc(dve1, 1)
                    dve.wait_ge(dve1, n[0])

                nc.vector.memset(ones[:, :], 1.0)
                nc.vector.memset(neg_half[:, :], -0.5)
                for g in G:
                    link(nc.vector.memset(g[:, :, :], 0.0))
                dve.wait_ge(cols, 2)
                nc.vector.tensor_copy(col[:, :], col_i[:, :])
                nc.vector.tensor_copy(colb[:, :], col_i[:, :])
                link(nc.vector.tensor_copy(row[:, 0:1], row_i[:, :]))
                nc.vector.tensor_scalar(row[:, 1:2], row[:, 0:1], float(P), None, ALU.add)
                nc.vector.tensor_scalar(ident[:, :], col[:, 0:P], row[:, 0:1], None, ALU.is_equal)
                nc.vector.tensor_scalar(before[:, :], col[:, 0:P], row[:, 0:1], None, ALU.is_gt)
                link(nc.vector.tensor_scalar(after[:, :], col[:, 0:P], row[:, 0:1], None, ALU.is_lt))
                dve.wait_ge(loaded, 16 * (len(CHALF) + (EL < P)))
                nc.vector.tensor_scalar(ints2[:, :, 0:P], ints[:, :, 0:P], 7, None, ALU.arith_shift_right)
                link(nc.vector.tensor_scalar(ints2[:, :, P:2 * P], ints[:, :, 0:P], P - 1, None, ALU.bitwise_and))
                nc.vector.tensor_copy(fl[:, :, :], ints2[:, :, :]).then_inc(turned, 1)
                dve.wait_ge(turned, 2)
                nc.vector.tensor_copy(hi_t[:, :], bank[0][:, 0:NC])
                link(nc.vector.tensor_copy(lo_t[:, :], bank[1][:, 0:NC]))
                def one_hot(t, known):
                    if known is None or known >= 4:
                        dve.wait_ge(hot_used, t.n - 3)
                    nc.vector.tensor_scalar(oh_lo[t.u][:, :], colb[:, 0:P], lo_t[:, bass.ds(t.n, 1)], None,
                                            ALU.is_equal).then_inc(hot_made, 1)
                    nc.vector.tensor_scalar(oh_hi[t.u][:, 0:NT], colb[:, 0:NT], hi_t[:, bass.ds(t.n, 1)], None,
                                            ALU.is_equal).then_inc(hot_made, 1)
                run_tiles(dve, NC, 4, one_hot)
                dve.wait_ge(counted, 1)
                nc.vector.tensor_copy(deg[:, :], bank[2][:, 0:NT])
                nc.vector.tensor_scalar(dinv2[:, :], bank[2][:, 0:NT], 1.0, None, ALU.add).then_inc(counted, 1)
                dve.wait_ge(counted, 3)
                link(nc.vector.memset(cnt[:, :], 0.0))
                dve.wait_ge(turned, 3)
                for h, rows in THALF:
                    c = nc.vector.tensor_copy(cnt[0:rows, h:h + 1], bank[3][0:rows, h:h + 1])
                c.then_inc(turned, 1)
                dve.wait_ge(counted, 4)
                nc.vector.tensor_copy(start_i[:, 0:len(THALF)], bank[4][:, 0:len(THALF)]).then_inc(counted, 1)
                dve.wait_ge(windows, 32 * len(THALF))
                link(nc.vector.memset(seen[:, :], 0.0))
                for h, rows in THALF:
                    r = slice(0, rows)
                    link(nc.vector.tensor_copy(fl2[r, h, :], ints[r, h, :]))
                    link(nc.vector.tensor_scalar(ints[r, h, :], ints[r, h, :], 7, None, ALU.arith_shift_right))
                    link(nc.vector.tensor_copy(fl[r, h, :], ints[r, h, :]))
                    link(nc.vector.scalar_tensor_tensor(fl2[r, h, :], fl[r, h, :], -float(P), fl2[r, h, :],
                                                        ALU.mult, ALU.add))
                    link(nc.vector.tensor_scalar(fl[r, h, :], fl[r, h, :], row[r, h:h + 1], None, ALU.is_equal))
                    link(nc.vector.scalar_tensor_tensor(fl[r, h, :], col[r, :], cnt[r, h:h + 1], fl[r, h, :],
                                                        ALU.is_lt, ALU.mult))
                    link(nc.vector.reduce_sum(seen[r, h:h + 1], fl[r, h, :], mybir.AxisListType.X))
                link(nc.vector.tensor_tensor(ok[:, 0:1], seen[:, 0:1], seen[:, 1:2], ALU.add))
                nc.vector.tensor_copy(ok[:, 0:1], ok[:, 0:1]).then_inc(turned, 1)
                dve.wait_ge(turned, 6)
                link(nc.vector.tensor_scalar(ok[:, 1:2], bank[5][:, 0:1], -2.0 if force_general else float(E), None, ALU.is_equal))
                nc.vector.tensor_scalar(general[:, :], ok[:, 1:2], -1.0, 1.0, ALU.mult, ALU.add)
                for h, rows in THALF:
                    r = slice(0, rows)
                    link(nc.vector.tensor_scalar(fl[r, h, :], fl[r, h, :], ok[r, 1:2], None, ALU.mult))
                    link(nc.vector.scalar_tensor_tensor(fl2[r, h, :], fl2[r, h, :], 1.0, fl[r, h, :],
                                                        ALU.add, ALU.mult))
                    link(nc.vector.tensor_scalar(fl2[r, h, :], fl2[r, h, :], -1.0, None, ALU.add))
                dve.wait_ge(windows, 32 * len(THALF))
                dve.wait_ge(turned, 6)
                nc.vector.tensor_copy(ok[:, 0:1], ok[:, 1:2]).then_inc(turned, 1)
                dve.wait_ge(turned, 8)
                for k in range(CHUNKS):
                    c = nc.vector.tensor_copy(edge_to[:, k, :], bank[6 + k][:, 0:NT])
                link(c)
                for h, rows in THALF:
                    r = slice(0, rows)
                    link(nc.vector.tensor_copy(fl2[r, h, :], ints2[r, h, :]))
                    link(nc.vector.scalar_tensor_tensor(fl2[r, h, :], fl2[r, h, :], -float(NOWHERE), fl[r, h, :],
                                                        ALU.add, ALU.mult))
                    link(nc.vector.tensor_scalar(fl2[r, h, :], fl2[r, h, :], float(NOWHERE), None, ALU.add))
                nc.vector.tensor_copy(ok[:, 0:1], ok[:, 1:2]).then_inc(turned, 1)
                dve.wait_ge(turned, 10)
                for k in range(CHUNKS):
                    c = nc.vector.tensor_copy(edge_from[:, k, :], bank[6 + k][:, 0:NT])
                for q in range(3):
                    for k in range(KD):
                        dve.wait_ge(w_split, KD * q + k + 1)
                        nc.vector.tensor_tensor(Wlo[q][:, k, :], stage[k][:, :], Whi[q][:, k, :].bitcast(F32),
                                                ALU.subtract).then_inc(w_free, 1)

            @block.tensor
            def _(pe):
                pe.wait_ge(turned, 1)
                pe.wait_ge(dve1, 5)
                for h, rows in CHALF:
                    nc.tensor.transpose(bank[0][:, h * P:h * P + rows], fl[0:rows, h, 0:P], ident[0:rows, 0:rows])
                    m = nc.tensor.transpose(bank[1][:, h * P:h * P + rows], fl[0:rows, h, P:2 * P],
                                            ident[0:rows, 0:rows])
                m.then_inc(turned, 1)

                def count(t, known):
                    pe.wait_ge(hot_made, 2 * t.n + 2)
                    m = nc.tensor.matmul(bank[2][:, 0:NT], oh_lo[t.u][:, :], oh_hi[t.u][:, 0:NT],
                                         start=(known == 0), stop=(known == NC - 1), skip_group_check=True)
                    m.then_inc(hot_used, 1)
                    if known == NC - 1:
                        pe.wait_ge(hot_used, NC)
                        nc.tensor.transpose(bank[7][0:P, 0:P], ident[:, :], ident[:, :]).then_inc(counted, 1)
                run_tiles(pe, NC, 4, count)
                pe.wait_ge(counted, 2)
                for h, rows in THALF:
                    m = nc.tensor.matmul(bank[3][0:rows, h:h + 1], deg[:, h * P:h * P + rows], ones[:, 0:1],
                                         start=True, stop=True, skip_group_check=True)
                m.then_inc(turned, 1)
                pe.wait_ge(turned, 4)
                for h, _ in THALF:
                    m = nc.tensor.matmul(bank[4][:, h:h + 1], before[:, :], cnt[:, h:h + 1], start=True, stop=(h == 0),
                                         skip_group_check=True)
                    if h:
                        m = nc.tensor.matmul(bank[4][:, h:h + 1], ones[:, :], cnt[:, 0:1], start=False, stop=True,
                                             skip_group_check=True)
                m.then_inc(counted, 1)
                pe.wait_ge(turned, 5)
                nc.tensor.matmul(bank[5][:, 0:1], ones[:, :], ok[:, 0:1], start=True, stop=True).then_inc(turned, 1)
                for after_step in (7, 9):
                    pe.wait_ge(turned, after_step)
                    for k in range(CHUNKS):
                        for h, rows in THALF:
                            m = nc.tensor.transpose(bank[6 + k][:, h * P:h * P + rows],
                                                    fl2[0:rows, h, k * P:(k + 1) * P], ident[0:rows, 0:rows])
                    m.then_inc(turned, 1)

        x_in = [sem(f"x_in{u}") for u in range(NORM_SLOTS)]
        h_out = [sem(f"h_out{u}") for u in range(NORM_SLOTS)]
        st_made, ag_made, ve_made, rs_made = sem("n_stats"), sem("n_mean_var"), sem("n_var_eps"), sem("n_rstd")
        sc_made, co_made, hn_made = sem("n_scale"), sem("n_coefs"), sem("n_h")
        NX = [*Self, *Xt]
        NH = [*Cv, *Y]

        def rows_of(known):
            return LAST if known == NT - 1 else P

        with nc.Block() as block:
            @block.sync
            def _(sp):
                def load(t, known):
                    r = rows_of(known)
                    if known is None or known >= NORM_SLOTS:
                        sp.wait_ge(hn_made, t.n - NORM_SLOTS + 1)
                    sp.dma_start(NX[t.u][0:r, :], x[bass.ds(t.n * P, r), :]).then_inc(x_in[t.u], 16)
                run_tiles(sp, NT, NORM_SLOTS, load)
                for u in range(NORM_SLOTS):
                    sp.wait_ge(x_in[u], 16 * len(range(u, NT, NORM_SLOTS)))

            @block.vector
            def _(dve):
                def keep(t):
                    m = small[t.u]
                    nc.vector.tensor_copy(rstd_x[:, bass.ds(t.n, 1)], m[:, 9:10])
                    nc.vector.scalar_tensor_tensor(nb_x[:, bass.ds(t.n, 1)], m[:, 6:7], -1.0, m[:, 9:10],
                                                   ALU.mult, ALU.mult)

                def coefs(t):
                    m = small[t.u]
                    nc.vector.tensor_tensor(m[:, 10:11], m[:, 9:10], dinv[:, bass.ds(t.n, 1)], ALU.mult)\
                        .then_inc(sc_made, 1)
                    dve.wait_ge(sc_made, t.n + 1)
                    nc.vector.scalar_tensor_tensor(m[:, 11:12], m[:, 6:7], -1.0, m[:, 10:11], ALU.mult, ALU.mult)\
                        .then_inc(co_made, 1)

                def stats(t, known):
                    m = small[t.u]
                    dve.wait_ge(x_in[t.u], 16 * (t.i + 1))
                    if known is None or known >= NORM_SLOTS:
                        dve.wait_ge(hn_made, t.n - NORM_SLOTS + 1)
                    nc.vector.bn_stats(m[:, 0:6], NX[t.u][:, :]).then_inc(st_made, 1)
                    if known != 0:
                        dve.wait_ge(rs_made, t.n)
                        dve.wait_ge(st_made, t.n + 1)
                        keep(t.after(-1))
                    else:
                        dve.wait_ge(st_made, 1)
                    nc.vector.bn_aggr(m[:, 6:8], m[:, 0:6]).then_inc(ag_made, 1)
                    if known != 0:
                        coefs(t.after(-1))
                    dve.wait_ge(ag_made, t.n + 1)
                    nc.vector.tensor_scalar(m[:, 8:9], m[:, 7:8], EPS, None, ALU.add).then_inc(ve_made, 1)
                    if known == NT - 1:
                        dve.wait_ge(rs_made, NT)
                        keep(t)
                        coefs(t)
                run_tiles(dve, NT, NORM_SLOTS, stats)

            @block.gpsimd
            def _(pool):
                def power(t, known):
                    m = small[t.u]
                    pool.wait_ge(ve_made, t.n + 1)
                    nc.gpsimd.tensor_tensor(m[:, 9:10], m[:, 8:9], neg_half[:, 0:1], ALU.pow).then_inc(rs_made, 1)
                run_tiles(pool, NT, NORM_SLOTS, power)

            @block.scalar
            def _(act):
                def store(t, known):
                    r = rows_of(known)
                    act.wait_ge(hn_made, t.n + 1)
                    act.dma_start(H[0][bass.ds(t.n * P, r), :], NH[t.u][0:r, :]).then_inc(h_out[t.u], 16)

                def normalise(t, known):
                    m = small[t.u]
                    act.wait_ge(co_made, t.n + 1)
                    if known is None or known >= NORM_SLOTS:
                        act.wait_ge(h_out[t.u], 16 * t.i)
                    nc.scalar.activation(NH[t.u][:, :], NX[t.u][:, :], ACT.Relu, bias=m[:, 11:12],
                                         scale=m[:, 10:11]).then_inc(hn_made, 1)
                    if known != 0:
                        store(t.after(-1), None)
                    if known == NT - 1:
                        store(t, known)
                run_tiles(act, NT, NORM_SLOTS, normalise)
                for u in range(NORM_SLOTS):
                    act.wait_ge(h_out[u], 16 * len(range(u, NT, NORM_SLOTS)))

        g_copied, g_idx, g_rows, g_add = sem("g_copied"), sem("g_indices"), sem("g_rows"), sem("g_added")
        g_step, g_sum, g_to, g_idle = sem("g_step"), sem("g_summed"), sem("g_targets"), sem("g_idle")
        idle = sb("idle", [P, 2])

        def general_sums(q):
            def k(c):
                return q * NC + c

            row_dst, M, Gs, Sum = Cv[0][:, 0:P], Cv[1], Y[0], Y[1]
            row_i32 = ints[:, 0, 0:P]
            def added(n):
                return n + q + 1

            def general_sync(sp):
                sp.dma_start(H[q][ROWS:ROWS + (NT - 1) * P, :], H[q][0:(NT - 1) * P, :]).then_inc(g_add, 16)
                sp.dma_start(H[q][ROWS + (NT - 1) * P:ROWS + N, :], H[q][(NT - 1) * P:N, :]).then_inc(g_copied, 16)
                for z in range(2):
                    sp.dma_start(H[q][ROWS + NP + z * P:ROWS + NP + (z + 1) * P, :], G[0][:, 0, :])\
                        .then_inc(g_copied, 16)
                sp.wait_ge(g_copied, 48 * (q + 1))
                with sp.Fori(0, NC) as c:
                    sp.wait_ge(g_add, 16 * added(k(c)))
                    sp.dma_start(ints2[:, 0, 0:1], SRC[bass.ds(c * P, P), :]).then_inc(g_idx, 16)
                    sp.dma_start(ints2[:, 0, 1:2], DST[bass.ds(c * P, P), :]).then_inc(g_idx, 16)
                    sp.dma_start(row_i32, DST[bass.ds(c * P, P), :].rearrange("j o -> o j").broadcast_to([P, P]))\
                        .then_inc(g_idx, 16)

            def general_pool(pool):
                def carry_wait(j):
                    nc.gpsimd.tensor_tensor(idle[:, j:j + 1], row[:, 0:1], row[:, 0:1], ALU.add).then_inc(g_idle, 1)

                last_row, last_sum = pool.to_reg(N - 1), pool.to_reg(2 * ROWS - 1)
                pool.wait_ge(g_copied, 48 * (q + 1))
                pool.wait_ge(g_add, 16 * added(k(0)))
                with pool.Fori(0, NC) as c:
                    pool.wait_ge(g_idx, 48 * (k(c) + 1))
                    carry_wait(0)
                    pool.indirect_dma_start(Gs[:, :], None, H[q][0:N, :],
                                            bass.IndirectOffsetOnAxis(ap=ints2[:, 0, 0:1], axis=0),
                                            bounds_check=last_row, oob_is_err=False).then_inc(g_rows, 16)
                    pool.wait_ge(g_to, k(c) + 1)
                    pool.wait_ge(g_idle, 2 * k(c) + 1)
                    carry_wait(1)
                    pool.indirect_dma_start(H[q], bass.IndirectOffsetOnAxis(ap=ints2[:, 1, 0:1], axis=0),
                                            Sum[:, :], None, bounds_check=last_sum,
                                            compute_op=ALU.add).then_inc(g_add, 16)
                pool.wait_ge(g_add, 16 * added(k(NC)))

            def general_vector(dve):
                with dve.Fori(0, NC) as c:
                    s = 7 * k(c)
                    dve.wait_ge(g_idx, 48 * (k(c) + 1))
                    nc.vector.tensor_copy(row_dst, row_i32)
                    nc.vector.tensor_copy(M[:, 2 * P:2 * P + 1], ints2[:, 0, 1:2]).then_inc(g_step, 1)
                    dve.wait_ge(g_step, s + 1)
                    nc.vector.tensor_scalar(M[:, 0:P], row_dst, M[:, 2 * P:2 * P + 1], None, ALU.is_equal)\
                        .then_inc(g_step, 1)
                    dve.wait_ge(g_step, s + 2)
                    nc.vector.tensor_tensor(M[:, P:2 * P], M[:, 0:P], after[:, :], ALU.mult).then_inc(g_step, 1)
                    dve.wait_ge(g_step, s + 3)
                    nc.vector.reduce_sum(M[:, 2 * P + 1:2 * P + 2], M[:, P:2 * P], mybir.AxisListType.X)\
                        .then_inc(g_step, 1)
                    dve.wait_ge(g_step, s + 4)
                    nc.vector.tensor_scalar(M[:, 2 * P + 2:2 * P + 3], M[:, 2 * P + 1:2 * P + 2], 0.0, None,
                                            ALU.is_equal)
                    nc.vector.tensor_scalar(M[:, 2 * P + 3:2 * P + 4], row[:, 0:1], -1.0, -float(TRASH),
                                            ALU.mult, ALU.add).then_inc(g_step, 1)
                    dve.wait_ge(g_step, s + 5)
                    nc.vector.tensor_tensor(M[:, 2 * P + 4:2 * P + 5], M[:, 2 * P:2 * P + 1],
                                            M[:, 2 * P + 3:2 * P + 4], ALU.add).then_inc(g_step, 1)
                    dve.wait_ge(g_step, s + 6)
                    nc.vector.scalar_tensor_tensor(M[:, 2 * P + 5:2 * P + 6], M[:, 2 * P + 4:2 * P + 5],
                                                   M[:, 2 * P + 2:2 * P + 3], M[:, 2 * P + 3:2 * P + 4],
                                                   ALU.mult, ALU.subtract).then_inc(g_step, 1)
                    dve.wait_ge(g_step, s + 7)
                    nc.vector.tensor_scalar(ints2[:, 1, 0:1], M[:, 2 * P + 5:2 * P + 6], float(ROWS), None,
                                            ALU.add)
                    dve.wait_ge(g_sum, k(c) + 1)
                    nc.vector.tensor_copy(Sum[:, :], bank[6][:, :]).then_inc(g_to, 1)
                dve.wait_ge(g_add, 16 * added(k(NC)))

            def general_tensor(pe):
                with pe.Fori(0, NC) as c:
                    pe.wait_ge(g_rows, 16 * (k(c) + 1))
                    pe.wait_ge(g_step, 7 * k(c) + 2)
                    nc.tensor.matmul(bank[6][:, :], M[:, 0:P], Gs[:, :], start=True, stop=True)\
                        .then_inc(g_sum, 1)

            return general_sync, general_pool, general_vector, general_tensor

        names = dict(
            self_in=[sem(f"self_in{u}") for u in range(SLOTS)],
            edge_in=[sem(f"edge_in{u}") for u in range(SLOTS)],
            xt_in=[sem(f"xt_in{u}") for u in range(SLOTS)],
            ho_out=[sem(f"ho_out{u}") for u in range(SLOTS)],
            xo_out=[sem(f"xo_out{u}") for u in range(SLOTS)],
        )
        self_in, edge_in, xt_in, ho_out, xo_out = names.values()
        idx_made = sem("idx_made")
        s_made = sem("s_made")
        agg_done, hi_done, lo_done, main_done = sem("agg_done"), sem("hi_done"), sem("lo_done"), sem("main_done")
        conv_done, stats_done, mv_done, ve_done = sem("conv_done"), sem("stats_done"), sem("mv_done"), sem("ve_done")
        rstd_done, cg_done, y_done, gelu_done = sem("rstd_done"), sem("cg_done"), sem("y_done"), sem("gelu_done")
        h_done, r_done, rb_done = sem("h_done"), sem("r_done"), sem("rb_done")
        x2_done, st2_done, mv2_done, ve2_done = sem("x2_done"), sem("st2_done"), sem("mv2_done"), sem("ve2_done")
        rs2_done, sc2_done, co2_done, xb_done, res_done = (sem("rs2_done"), sem("sc2_done"), sem("co2_done"),
                                                           sem("xb_done"), sem("res_done"))

        def convolution(q):
            first, second, third = q == 0, q == 1, q == 2

            def uses(t, a_phase=q):
                return a_phase * len(range(t.u, NT, SLOTS)) + t.i + 1

            def upto(t, phase=q):
                return phase * NT + t.n + 1

            def wait_free(engine, s, t, known, phase=q):
                if known is not None and known < SLOTS:
                    if phase:
                        engine.wait_ge(s, phase * NT)
                else:
                    engine.wait_ge(s, phase * NT + t.n - SLOTS + 1)

            def shifted(known, k):
                return None if known is None else known + k

            general_sync, general_pool, general_vector, general_tensor = general_sums(q)

            def if_general(engine, program):
                flag = engine.value_load(general[0:1, 0:1], min_val=0, max_val=1)
                with engine.If(flag > 0):
                    program(engine)
                return flag

            with nc.Block() as block:
                @block.sync
                def _(sp):
                    general_reg = if_general(sp, general_sync)

                    def load(t, known):
                        r = rows_of(known)
                        wait_free(sp, agg_done, t, known)
                        sp.dma_start(Self[t.u][0:r, :], H[q][bass.ds(general_reg * ROWS + t.n * P, r), :])\
                            .then_inc(self_in[t.u], 16)
                        if second:
                            wait_free(sp, x2_done, t, known, 0)
                            sp.dma_start(Xt[t.u][0:r, :], x[bass.ds(t.n * P, r), :]).then_inc(xt_in[t.u], 16)
                        if third:
                            wait_free(sp, xb_done, t, known, 0)
                            sp.dma_start(Xt[t.u][0:r, :], X2[bass.ds(t.n * P, r), :]).then_inc(xt_in[t.u], 16)

                    def store(t, known):
                        r = rows_of(known)
                        if first:
                            sp.wait_ge(h_done, upto(t))
                            sp.dma_start(H[1][bass.ds(t.n * P, r), :], Ho[t.u][0:r, :]).then_inc(ho_out[t.u], 16)
                        if second:
                            sp.wait_ge(x2_done, upto(t, 0))
                            sp.dma_start(X2[bass.ds(t.n * P, r), :], X2t[t.u][0:r, :]).then_inc(xo_out[t.u], 16)
                            sp.wait_ge(h_done, upto(t))
                            sp.dma_start(H[2][bass.ds(t.n * P, r), :], Ho[t.u][0:r, :]).then_inc(ho_out[t.u], 16)
                        if third:
                            sp.wait_ge(res_done, upto(t, 0))
                            sp.dma_start(out[bass.ds(t.n * P, r), :], Cv[t.u][0:r, :]).then_inc(xo_out[t.u], 16)

                    def body(t, known):
                        if known == 0:
                            load(t, 0)
                            load(t.after(1), 1)
                        if known is None or known + 2 < NT:
                            load(t.after(2), shifted(known, 2))
                        if known != 0:
                            store(t.after(-1), shifted(known, -1))
                        if known == NT - 1:
                            store(t, known)
                    run_tiles(sp, NT, SLOTS, body)
                    for u in range(SLOTS):
                        n = len(range(u, NT, SLOTS))
                        if not third:
                            sp.wait_ge(ho_out[u], 16 * (q + 1) * n)
                        if not first:
                            sp.wait_ge(xo_out[u], 16 * q * n)

                @block.gpsimd
                def _(pool):
                    if_general(pool, general_pool)

                    def indices(t, known):
                        if known is None or known >= SLOTS:
                            pool.wait_ge(edge_in[t.u], 16 * CHUNKS * (uses(t) - 1))
                        nc.gpsimd.tensor_copy(idx[t.u][:, :], edge_from[:, :, bass.ds(t.n, 1)]
                                              .rearrange("p k o -> p (k o)")).then_inc(idx_made, 1)

                    def gather(t, known, between=None):
                        wait_free(pool, agg_done, t, known)
                        pool.wait_ge(idx_made, upto(t))
                        if between:
                            between()
                        for k in range(CHUNKS):
                            pool.indirect_dma_start(G[t.u][:, k, :], None, H[q][0:N, :],
                                                    bass.IndirectOffsetOnAxis(ap=idx[t.u][:, k:k + 1], axis=0),
                                                    bounds_check=N - 1, oob_is_err=False).then_inc(edge_in[t.u], 16)

                    def late(t):
                        if second:
                            pool.wait_ge(ve2_done, upto(t, 0))
                            m = small2[t.u]
                            nc.gpsimd.tensor_tensor(m[:, 9:10], m[:, 8:9], neg_half[:, 0:1], ALU.pow)\
                                .then_inc(rs2_done, 1)

                    def body(t, known):
                        if known == 0:
                            for k in range(SLOTS):
                                indices(t.after(k), k)
                            gather(t, 0)
                            gather(t.after(1), 1)
                        next_indices = None
                        if known is None or known + 3 < NT:
                            def next_indices():
                                indices(t.after(3), shifted(known, 3))
                        if known is None or known + 2 < NT:
                            gather(t.after(2), shifted(known, 2), next_indices)
                        if second:
                            pool.wait_ge(r_done, upto(t, 0))
                            nc.gpsimd.tensor_tensor(R[t.u][:, :], R[t.u][:, :], beta_b[1][:, :], ALU.add)\
                                .then_inc(rb_done, 1)
                        if third:
                            pool.wait_ge(xt_in[t.u], 16 * (uses(t, 1)))
                            wait_free(pool, res_done, t, known, 0)
                            nc.gpsimd.tensor_tensor(R[t.u][:, :], Xt[t.u][:, :], bias_b[2][:, :], ALU.add)\
                                .then_inc(xb_done, 1)
                        if known != 0:
                            late(t.after(-1))
                        if not third:
                            m = small[t.u]
                            pool.wait_ge(ve_done, upto(t))
                            nc.gpsimd.tensor_tensor(m[:, 9:10], m[:, 8:9], neg_half[:, 0:1], ALU.pow)\
                                .then_inc(rstd_done, 1)
                        if known == NT - 1:
                            late(t)
                    run_tiles(pool, NT, SLOTS, body)

                @block.scalar
                def _(act):
                    def high(t):
                        act.wait_ge(agg_done, upto(t))
                        nc.scalar.activation(Ahi[t.u][:, :], Agg[t.u][:, :], ACT.Copy).then_inc(hi_done, 1)

                    def late(t, known):
                        if second:
                            m = small2[t.u]
                            act.wait_ge(co2_done, upto(t, 0))
                            if known is None or known >= SLOTS:
                                act.wait_ge(ho_out[t.u], 16 * (uses(t) - 1))
                            nc.scalar.activation(Ho[t.u][:, :], X2t[t.u][:, :], ACT.Relu, bias=m[:, 11:12],
                                                 scale=m[:, 10:11]).then_inc(h_done, 1)

                    def body(t, known):
                        if known == 0:
                            high(t)
                        if known != NT - 1:
                            high(t.after(1))
                        if second:
                            act.wait_ge(xt_in[t.u], 16 * uses(t, 0))
                            wait_free(act, y_done, t, known)
                            nc.scalar.activation(R[t.u][:, :], Xt[t.u][:, :], ACT.Relu,
                                                 bias=nb_x[:, bass.ds(t.n, 1)],
                                                 scale=rstd_x[:, bass.ds(t.n, 1)]).then_inc(r_done, 1)
                        if known != 0:
                            late(t.after(-1), shifted(known, -1))
                        if not third:
                            act.wait_ge(y_done, upto(t))
                            nc.scalar.activation(Y[t.u][:, :], Y[t.u][:, :], ACT.Gelu).then_inc(gelu_done, 1)
                        if first:
                            if known is None or known >= SLOTS:
                                act.wait_ge(ho_out[t.u], 16 * (uses(t) - 1))
                            act.wait_ge(gelu_done, upto(t))
                            nc.scalar.activation(Ho[t.u][:, :], Y[t.u][:, :], ACT.Copy,
                                                 scale=dinv[:, bass.ds(t.n, 1)]).then_inc(h_done, 1)
                        if known == NT - 1:
                            late(t, known)
                    run_tiles(act, NT, SLOTS, body)

                @block.vector
                def _(dve):
                    if_general(dve, general_vector)

                    def select(t, known):
                        if known is not None:
                            wait_free(dve, agg_done, t, known)
                        for k in range(CHUNKS):
                            i = nc.vector.tensor_scalar(S[t.u][:, k, :], col[:, 0:P], edge_to[:, k, bass.ds(t.n, 1)],
                                                        None, ALU.is_equal)
                        i.then_inc(s_made, 1)

                    def low(t):
                        dve.wait_ge(hi_done, upto(t))
                        nc.vector.tensor_tensor(Alo[t.u][:, :], Agg[t.u][:, :], Ahi[t.u][:, :].bitcast(F32),
                                                ALU.subtract).then_inc(lo_done, 1)

                    def late(t, known, between):
                        m = small2[t.u]
                        dve.wait_ge(gelu_done, upto(t))
                        if known is None or known >= SLOTS:
                            dve.wait_ge(xo_out[t.u], 16 * (uses(t, 0) - 1))
                            dve.wait_ge(h_done, upto(t) - SLOTS)
                        nc.vector.tensor_tensor(X2t[t.u][:, :], Xt[t.u][:, :], Y[t.u][:, :], ALU.add)\
                            .then_inc(x2_done, 1)
                        dve.wait_ge(x2_done, upto(t, 0))
                        nc.vector.bn_stats(m[:, 0:6], X2t[t.u][:, :]).then_inc(st2_done, 1)
                        dve.wait_ge(st2_done, upto(t, 0))
                        between()
                        nc.vector.bn_aggr(m[:, 6:8], m[:, 0:6]).then_inc(mv2_done, 1)
                        dve.wait_ge(mv2_done, upto(t, 0))
                        nc.vector.tensor_scalar(m[:, 8:9], m[:, 7:8], EPS, None, ALU.add).then_inc(ve2_done, 1)

                    def late_coefs(t):
                        m = small2[t.u]
                        dve.wait_ge(rs2_done, upto(t, 0))
                        nc.vector.tensor_tensor(m[:, 10:11], m[:, 9:10], dinv[:, bass.ds(t.n, 1)], ALU.mult)\
                            .then_inc(sc2_done, 1)
                        dve.wait_ge(sc2_done, upto(t, 0))
                        nc.vector.scalar_tensor_tensor(m[:, 11:12], m[:, 6:7], -1.0, m[:, 10:11], ALU.mult, ALU.mult)\
                            .then_inc(co2_done, 1)

                    def body(t, known):
                        m = small[t.u]
                        if known == 0:
                            select(t, 0)
                            select(t.after(1), 1)
                            select(t.after(2), 2)
                            low(t)

                        def low_next():
                            if known != NT - 1:
                                low(t.after(1))
                        if second and known != 0:
                            late(t.after(-1), shifted(known, -1), low_next)
                        else:
                            low_next()
                        dve.wait_ge(main_done, upto(t))
                        if third:
                            dve.wait_ge(xb_done, upto(t, 0))
                            if known is None or known >= SLOTS:
                                dve.wait_ge(xo_out[t.u], 16 * (uses(t, 1) - 1))
                            nc.vector.scalar_tensor_tensor(Cv[t.u][:, :], Out[t.u][:, :], dinv[:, bass.ds(t.n, 1)],
                                                           R[t.u][:, :], ALU.mult, ALU.add).then_inc(res_done, 1)
                            if known is None or known + 3 < NT:
                                wait_free(dve, agg_done, t.after(3), shifted(known, 3))
                                select(t.after(3), None)
                            return
                        nc.vector.scalar_tensor_tensor(Cv[t.u][:, :], Out[t.u][:, :], dinv[:, bass.ds(t.n, 1)],
                                                       bias_b[q][:, :], ALU.mult, ALU.add).then_inc(conv_done, 1)
                        if second and known != 0:
                            late_coefs(t.after(-1))
                        dve.wait_ge(conv_done, upto(t))
                        nc.vector.bn_stats(m[:, 0:6], Cv[t.u][:, :]).then_inc(stats_done, 1)
                        if known is None or known + 3 < NT:
                            wait_free(dve, agg_done, t.after(3), shifted(known, 3))
                            dve.wait_ge(stats_done, upto(t))
                            select(t.after(3), None)
                        else:
                            dve.wait_ge(stats_done, upto(t))
                        nc.vector.bn_aggr(m[:, 6:8], m[:, 0:6]).then_inc(mv_done, 1)
                        dve.wait_ge(mv_done, upto(t))
                        nc.vector.tensor_scalar(m[:, 8:9], m[:, 7:8], EPS, None, ALU.add).then_inc(ve_done, 1)
                        nc.vector.scalar_tensor_tensor(Cv[t.u][:, :], Cv[t.u][:, :], m[:, 6:7], gamma_b[q][:, :],
                                                       ALU.subtract, ALU.mult).then_inc(cg_done, 1)
                        dve.wait_ge(rstd_done, upto(t))
                        dve.wait_ge(cg_done, upto(t))
                        if first:
                            wait_free(dve, h_done, t, known)
                            plus = beta_b[0]
                        else:
                            dve.wait_ge(rb_done, upto(t, 0))
                            plus = R[t.u]
                        nc.vector.scalar_tensor_tensor(Y[t.u][:, :], Cv[t.u][:, :], m[:, 9:10], plus[:, :],
                                                       ALU.mult, ALU.add).then_inc(y_done, 1)
                        if known == NT - 1:
                            if second:
                                late(t, known, lambda: None)
                                late_coefs(t)
                    run_tiles(dve, NT, SLOTS, body)

                @block.tensor
                def _(pe):
                    if_general(pe, general_tensor)

                    def aggregate(t, known):
                        pe.wait_ge(self_in[t.u], 16 * uses(t))
                        pe.wait_ge(edge_in[t.u], 16 * CHUNKS * uses(t))
                        pe.wait_ge(s_made, upto(t))
                        for f in range(KD):
                            fs = slice(f * P, (f + 1) * P)
                            nc.tensor.matmul(Agg[t.u][:, fs], Self[t.u][:, fs], ident[:, :], is_transpose=True,
                                             start=True, stop=False, skip_group_check=True)
                            for k in range(CHUNKS):
                                m = nc.tensor.matmul(Agg[t.u][:, fs], G[t.u][:, k, fs], S[t.u][:, k, :],
                                                     start=False, stop=(k == CHUNKS - 1), skip_group_check=True)
                        m.then_inc(agg_done, 1)

                    def multiply(t, known):
                        pe.wait_ge(hi_done, upto(t))
                        if not third:
                            wait_free(pe, conv_done, t, known)
                        else:
                            if known is not None and known < SLOTS:
                                pe.wait_ge(conv_done, 2 * NT)
                            else:
                                pe.wait_ge(res_done, t.n - SLOTS + 1)
                        n = 0
                        for a, w in ((Ahi, Whi), (Ahi, Wlo), (Alo, Whi)):
                            if a is Alo:
                                pe.wait_ge(lo_done, upto(t))
                            for f in range(KD):
                                m = nc.tensor.matmul(Out[t.u][:, :], a[t.u][:, f * P:(f + 1) * P], w[q][:, f, :],
                                                     start=(n == 0), stop=(n == 3 * KD - 1))
                                n += 1
                        m.then_inc(main_done, 1)

                    def body(t, known):
                        if known == 0:
                            aggregate(t, 0)
                        if known != NT - 1:
                            aggregate(t.after(1), shifted(known, 1))
                        multiply(t, known)
                    run_tiles(pe, NT, SLOTS, body)

        for q in range(3):
            convolution(q)


_INS = ['x', 'src', 'dst', 'L0_gnn_W1', 'L0_gnn_b1', 'L0_gnn_gamma1', 'L0_gnn_beta1', 'L0_gnn_W2', 'L0_gnn_b2',
        'L0_gnn_gamma2', 'L0_gnn_beta2', 'L1_gnn_W', 'L1_gnn_b']


def kernel(**inputs):
    import numpy as _np
    import concourse.bacc as _bacc
    from concourse import mybir as _mybir
    from concourse.bass_utils import run_bass_kernel_spmd as _run

    nc = _bacc.Bacc("TRN2", target_bir_lowering=False, num_devices=1)
    arrays, args = {}, []
    for name in _INS:
        a = _np.ascontiguousarray(inputs[name])
        arrays[f"in_{name}_dram"] = a
        args.append(nc.dram_tensor(f"in_{name}_dram", a.shape, _mybir.dt.from_np(a.dtype), kind="ExternalInput").ap())
    out = nc.dram_tensor("out_0_dram", inputs["x"].shape, _mybir.dt.float32, kind="ExternalOutput").ap()
    gnn_kernel(nc, *args, out)
    r = _run(nc, [arrays], core_ids=[0])
    return r.results[0]["out_0_dram"]
```

```python
from contextlib import ExitStack

import concourse.bass as bass
from concourse import mybir

P = 128
ALU = mybir.AluOpType
ACT = mybir.ActivationFunctionType
F32 = mybir.dt.float32
F32R = mybir.dt.float32r
BF16 = mybir.dt.bfloat16
I32 = mybir.dt.int32

EPS = 1e-5
SLOTS = 3
NORM_SLOTS = 6
CHUNKS = 2
WINDOW = CHUNKS * P
NOWHERE = 1 << 16


class Tile:

    def __init__(self, i, u, slots):
        self.i, self.u, self.slots = i, u, slots

    @property
    def n(self):
        return self.i * self.slots + self.u

    def after(self, k):
        return Tile(self.i + (self.u + k) // self.slots, (self.u + k) % self.slots, self.slots)


def run_tiles(engine, count, slots, body):
    rounds = (count - 1) // slots
    last = rounds - 1 if rounds > 2 else 1
    for n in range(slots):
        body(Tile(0, n, slots), n)
    if last > 1:
        with engine.Fori(1, last) as i:
            for u in range(slots):
                body(Tile(i, u, slots), None)
    for n in range(last * slots, count):
        body(Tile(n // slots, n % slots, slots), n)


def gnn_kernel(nc, x, src, dst, W1, b1, g1, be1, W2, b2, g2, be2, W3, b3, out, force_general=False):
    N, D = x.shape
    E = src.shape[0]
    NT = -(-N // P)
    NP = NT * P
    LAST = N - (NT - 1) * P
    NC = -(-E // P)
    EL = E - (NC - 1) * P
    KD = D // P
    THALF = [(h, min(P, NT - h * P)) for h in range(-(-NT // P))]
    CHALF = [(h, min(P, NC - h * P)) for h in range(-(-NC // P))]
    TRASH = NP + P
    ROWS = NP + 2 * P
    assert D == 512 and NT <= 2 * P and NC <= 2 * P and NT > 3 * SLOTS

    with ExitStack() as ctx:
        def sb(name, shape, dt=F32):
            return ctx.enter_context(nc.sbuf_tensor(name, shape, dt))

        def sem(name):
            return ctx.enter_context(nc.semaphore(name))

        def scratch(name, shape, dt=F32):
            return nc.dram_tensor(name, shape, dt, kind="Internal").ap()

        H = [scratch(f"H{q}", (2 * ROWS, D)) for q in range(3)]
        X2 = scratch("X2", (NP, D))
        SRC = scratch("src_padded", (E + 2 * WINDOW, 1), I32)
        DST = scratch("dst_padded", (E + 2 * WINDOW, 1), I32)

        ident = sb("ident", [P, P])
        ones = sb("ones", [P, P])
        before = sb("before", [P, P])
        after = sb("after", [P, P])
        col_i = sb("col_i", [P, 2 * P], I32)
        row_i = sb("row_i", [P, 1], I32)
        col = sb("col", [P, 2 * P])
        colb = sb("colb", [P, 2 * P], BF16)
        row = sb("row", [P, 2])
        neg_half = sb("neg_half", [P, 2 * P])
        dinv = sb("dinv", [P, NT])
        dinv2 = sb("dinv2", [P, NT])
        edge_to = sb("edge_to", [P, CHUNKS, NT])
        edge_from = sb("edge_from", [P, CHUNKS, NT], I32)
        rstd_x = sb("rstd_x", [P, NT])
        nb_x = sb("nb_x", [P, NT])
        general = sb("general", [P, 1], I32)
        Whi = [sb(f"Whi{q}", [P, KD, D], F32R) for q in range(3)]
        Wlo = [sb(f"Wlo{q}", [P, KD, D], F32R) for q in range(3)]
        vecs = [sb(f"vec{k}", [P, D]) for k in range(7)]
        bias_b, gamma_b, beta_b = vecs[0:3], vecs[3:5], vecs[5:7]

        Self = [sb(f"self{u}", [P, D]) for u in range(SLOTS)]
        G = [sb(f"g{u}", [P, CHUNKS, D]) for u in range(SLOTS)]
        S = [sb(f"s{u}", [P, CHUNKS, P]) for u in range(SLOTS)]
        Ahi = [sb(f"ahi{u}", [P, D], F32R) for u in range(SLOTS)]
        Alo = [sb(f"alo{u}", [P, D], F32R) for u in range(SLOTS)]
        Cv = [sb(f"conv{u}", [P, D]) for u in range(SLOTS)]
        Y = [sb(f"y{u}", [P, D]) for u in range(SLOTS)]
        Xt = [sb(f"x{u}", [P, D]) for u in range(SLOTS)]
        R = [sb(f"r{u}", [P, D]) for u in range(SLOTS)]
        X2t = [sb(f"x2{u}", [P, D]) for u in range(SLOTS)]
        Ho = [sb(f"ho{u}", [P, D]) for u in range(SLOTS)]
        small = [sb(f"small{u}", [P, 32]) for u in range(NORM_SLOTS)]
        idx = [sb(f"idx{u}", [P, CHUNKS], I32) for u in range(SLOTS)]

        bank = [ctx.enter_context(nc.psum_tensor(f"bank{b}", [P, 512], F32)) for b in range(8)]
        Agg, Out = bank[0:SLOTS], bank[SLOTS:2 * SLOTS]

        step = sem("prep_step")
        done = [0]

        def then(ins):
            done[0] += 1
            ins.then_inc(step, 1)
            return done[0]

        ints = sb("ints", [P, 2, WINDOW], I32)
        ints2 = sb("ints2", [P, 2, WINDOW], I32)
        fl = sb("fl", [P, 2, WINDOW])
        fl2 = sb("fl2", [P, 2, WINDOW])
        lo_t = sb("lo_t", [P, NC])
        hi_t = sb("hi_t", [P, NC])
        deg = sb("deg", [P, NT])
        oh_lo = [sb(f"oh_lo{u}", [P, P], BF16) for u in range(4)]
        oh_hi = [sb(f"oh_hi{u}", [P, 2 * P], BF16) for u in range(4)]
        cnt = sb("cnt", [P, 2])
        start_i = sb("start_i", [P, 2], I32)
        seen = sb("seen", [P, 2])
        ok = sb("ok", [P, 2])
        pad_i = sb("pad_i", [2, WINDOW], I32)

        loaded = sem("edges_loaded")
        weights = sem("weights_loaded")
        padded = sem("edges_padded")
        pads = sem("pads_written")
        consts = sem("consts_made")
        cols = sem("columns_made")
        dve1 = sem("dve_step")
        w_split = sem("weights_split")
        w_free = sem("weights_staged_free")
        turned = sem("edges_turned")
        hot_made = sem("one_hots_made")
        hot_used = sem("one_hots_used")
        counted = sem("degrees_counted")
        windows = sem("windows_fetched")

        stage = [Self[0], Self[1], Self[2], Xt[0]]

        with nc.Block() as block:
            @block.sync
            def _(sp):
                sp.wait_ge(consts, 1)
                for h, rows in CHALF:
                    full = rows if h < len(CHALF) - 1 or EL == P else rows - 1
                    sp.dma_start(ints[0:full, h, 0:P],
                                 dst[h * P * P:(h * P + full) * P].rearrange("(c j) -> c j", j=P)).then_inc(loaded, 16)
                    if full < rows:
                        sp.dma_start(ints[full:rows, h, 0:EL],
                                     dst[(NC - 1) * P:E].rearrange("(a j) -> a j", a=1)).then_inc(loaded, 16)
                for a, b in ((src, SRC), (dst, DST)):
                    r = next(k for k in (16, 15, 12, 10, 8, 6, 5, 4, 3, 2, 1) if E % k == 0)
                    sp.dma_start(b[0:E, :].rearrange("(a j) o -> a (j o)", a=r),
                                 a.rearrange("(a j) -> a j", a=r)).then_inc(padded, 16)
                sp.wait_ge(pads, 1)
                sp.dma_start(SRC[E:E + 2 * WINDOW, :].rearrange("(a j) o -> a (j o)", a=2), pad_i[:, :])\
                    .then_inc(padded, 16)
                sp.wait_ge(padded, 48)
                sp.wait_ge(pads, 2)
                sp.dma_start(DST[E:E + 2 * WINDOW, :].rearrange("(a j) o -> a (j o)", a=2), pad_i[:, :])\
                    .then_inc(padded, 16)
                for k, v in enumerate((b1, b2, b3, g1, g2, be1, be2)):
                    sp.dma_start(vecs[k][:, :], v.rearrange("(a d) -> a d", a=1).broadcast_to([P, D]))\
                        .then_inc(weights, 16)
                for q, w in enumerate((W1, W2, W3)):
                    wv = w.rearrange("(k p) n -> k p n", p=P)
                    if q:
                        sp.wait_ge(w_free, 4 * q)
                    for k in range(KD):
                        sp.dma_start(stage[k][:, :], wv[k, :, :]).then_inc(weights, 16)
                sp.wait_ge(weights, 16 * (7 + 3 * KD))
                sp.wait_ge(padded, 64)

            @block.gpsimd
            def _(pool):
                nc.gpsimd.memset(ints[:, :, :], -1).then_inc(consts, 1)
                nc.gpsimd.iota(col_i[:, :], pattern=[[1, 2 * P]], base=0, channel_multiplier=0).then_inc(cols, 1)
                nc.gpsimd.iota(row_i[:, :], pattern=[[0, 1]], base=0, channel_multiplier=1).then_inc(cols, 1)
                nc.gpsimd.memset(pad_i[:, :], 0).then_inc(pads, 1)
                pool.wait_ge(padded, 48)
                nc.gpsimd.memset(pad_i[:, :], NP).then_inc(pads, 1)
                pool.wait_ge(counted, 2)
                nc.gpsimd.tensor_tensor(dinv[:, :], dinv2[:, :], neg_half[:, 0:NT], ALU.pow).then_inc(counted, 1)
                pool.wait_ge(counted, 5)
                pool.wait_ge(padded, 64)
                for h, rows in THALF:
                    for a, o in ((SRC, ints2), (DST, ints)):
                        pool.indirect_dma_start(
                            o[0:rows, h, :], None, a,
                            bass.IndirectOffsetOnAxis(ap=start_i[0:rows, h:h + 1], axis=0),
                            bounds_check=E, oob_is_err=False).then_inc(windows, 16)

            @block.scalar
            def _(act):
                for q in range(3):
                    for k in range(KD):
                        act.wait_ge(weights, 16 * (7 + KD * (q + 1)))
                        nc.scalar.activation(Whi[q][:, k, :], stage[k][:, :], ACT.Copy).then_inc(w_split, 1)

            @block.vector
            def _(dve):
                n = [0]

                def link(ins):
                    n[0] += 1
                    ins.then_inc(dve1, 1)
                    dve.wait_ge(dve1, n[0])

                nc.vector.memset(ones[:, :], 1.0)
                nc.vector.memset(neg_half[:, :], -0.5)
                for g in G:
                    link(nc.vector.memset(g[:, :, :], 0.0))
                dve.wait_ge(cols, 2)
                nc.vector.tensor_copy(col[:, :], col_i[:, :])
                nc.vector.tensor_copy(colb[:, :], col_i[:, :])
                link(nc.vector.tensor_copy(row[:, 0:1], row_i[:, :]))
                nc.vector.tensor_scalar(row[:, 1:2], row[:, 0:1], float(P), None, ALU.add)
                nc.vector.tensor_scalar(ident[:, :], col[:, 0:P], row[:, 0:1], None, ALU.is_equal)
                nc.vector.tensor_scalar(before[:, :], col[:, 0:P], row[:, 0:1], None, ALU.is_gt)
                link(nc.vector.tensor_scalar(after[:, :], col[:, 0:P], row[:, 0:1], None, ALU.is_lt))
                dve.wait_ge(loaded, 16 * (len(CHALF) + (EL < P)))
                nc.vector.tensor_scalar(ints2[:, :, 0:P], ints[:, :, 0:P], 7, None, ALU.arith_shift_right)
                link(nc.vector.tensor_scalar(ints2[:, :, P:2 * P], ints[:, :, 0:P], P - 1, None, ALU.bitwise_and))
                nc.vector.tensor_copy(fl[:, :, :], ints2[:, :, :]).then_inc(turned, 1)
                dve.wait_ge(turned, 2)
                nc.vector.tensor_copy(hi_t[:, :], bank[0][:, 0:NC])
                link(nc.vector.tensor_copy(lo_t[:, :], bank[1][:, 0:NC]))
                def one_hot(t, known):
                    if known is None or known >= 4:
                        dve.wait_ge(hot_used, t.n - 3)
                    nc.vector.tensor_scalar(oh_lo[t.u][:, :], colb[:, 0:P], lo_t[:, bass.ds(t.n, 1)], None,
                                            ALU.is_equal).then_inc(hot_made, 1)
                    nc.vector.tensor_scalar(oh_hi[t.u][:, 0:NT], colb[:, 0:NT], hi_t[:, bass.ds(t.n, 1)], None,
                                            ALU.is_equal).then_inc(hot_made, 1)
                run_tiles(dve, NC, 4, one_hot)
                dve.wait_ge(counted, 1)
                nc.vector.tensor_copy(deg[:, :], bank[2][:, 0:NT])
                nc.vector.tensor_scalar(dinv2[:, :], bank[2][:, 0:NT], 1.0, None, ALU.add).then_inc(counted, 1)
                dve.wait_ge(counted, 3)
                link(nc.vector.memset(cnt[:, :], 0.0))
                dve.wait_ge(turned, 3)
                for h, rows in THALF:
                    c = nc.vector.tensor_copy(cnt[0:rows, h:h + 1], bank[3][0:rows, h:h + 1])
                c.then_inc(turned, 1)
                dve.wait_ge(counted, 4)
                nc.vector.tensor_copy(start_i[:, 0:len(THALF)], bank[4][:, 0:len(THALF)]).then_inc(counted, 1)
                dve.wait_ge(windows, 32 * len(THALF))
                link(nc.vector.memset(seen[:, :], 0.0))
                for h, rows in THALF:
                    r = slice(0, rows)
                    link(nc.vector.tensor_copy(fl2[r, h, :], ints[r, h, :]))
                    link(nc.vector.tensor_scalar(ints[r, h, :], ints[r, h, :], 7, None, ALU.arith_shift_right))
                    link(nc.vector.tensor_copy(fl[r, h, :], ints[r, h, :]))
                    link(nc.vector.scalar_tensor_tensor(fl2[r, h, :], fl[r, h, :], -float(P), fl2[r, h, :],
                                                        ALU.mult, ALU.add))
                    link(nc.vector.tensor_scalar(fl[r, h, :], fl[r, h, :], row[r, h:h + 1], None, ALU.is_equal))
                    link(nc.vector.scalar_tensor_tensor(fl[r, h, :], col[r, :], cnt[r, h:h + 1], fl[r, h, :],
                                                        ALU.is_lt, ALU.mult))
                    link(nc.vector.reduce_sum(seen[r, h:h + 1], fl[r, h, :], mybir.AxisListType.X))
                link(nc.vector.tensor_tensor(ok[:, 0:1], seen[:, 0:1], seen[:, 1:2], ALU.add))
                nc.vector.tensor_copy(ok[:, 0:1], ok[:, 0:1]).then_inc(turned, 1)
                dve.wait_ge(turned, 6)
                link(nc.vector.tensor_scalar(ok[:, 1:2], bank[5][:, 0:1], -2.0 if force_general else float(E), None, ALU.is_equal))
                nc.vector.tensor_scalar(general[:, :], ok[:, 1:2], -1.0, 1.0, ALU.mult, ALU.add)
                for h, rows in THALF:
                    r = slice(0, rows)
                    link(nc.vector.tensor_scalar(fl[r, h, :], fl[r, h, :], ok[r, 1:2], None, ALU.mult))
                    link(nc.vector.scalar_tensor_tensor(fl2[r, h, :], fl2[r, h, :], 1.0, fl[r, h, :],
                                                        ALU.add, ALU.mult))
                    link(nc.vector.tensor_scalar(fl2[r, h, :], fl2[r, h, :], -1.0, None, ALU.add))
                dve.wait_ge(windows, 32 * len(THALF))
                dve.wait_ge(turned, 6)
                nc.vector.tensor_copy(ok[:, 0:1], ok[:, 1:2]).then_inc(turned, 1)
                dve.wait_ge(turned, 8)
                for k in range(CHUNKS):
                    c = nc.vector.tensor_copy(edge_to[:, k, :], bank[6 + k][:, 0:NT])
                link(c)
                for h, rows in THALF:
                    r = slice(0, rows)
                    link(nc.vector.tensor_copy(fl2[r, h, :], ints2[r, h, :]))
                    link(nc.vector.scalar_tensor_tensor(fl2[r, h, :], fl2[r, h, :], -float(NOWHERE), fl[r, h, :],
                                                        ALU.add, ALU.mult))
                    link(nc.vector.tensor_scalar(fl2[r, h, :], fl2[r, h, :], float(NOWHERE), None, ALU.add))
                nc.vector.tensor_copy(ok[:, 0:1], ok[:, 1:2]).then_inc(turned, 1)
                dve.wait_ge(turned, 10)
                for k in range(CHUNKS):
                    c = nc.vector.tensor_copy(edge_from[:, k, :], bank[6 + k][:, 0:NT])
                for q in range(3):
                    for k in range(KD):
                        dve.wait_ge(w_split, KD * q + k + 1)
                        nc.vector.tensor_tensor(Wlo[q][:, k, :], stage[k][:, :], Whi[q][:, k, :].bitcast(F32),
                                                ALU.subtract).then_inc(w_free, 1)

            @block.tensor
            def _(pe):
                pe.wait_ge(turned, 1)
                pe.wait_ge(dve1, 5)
                for h, rows in CHALF:
                    nc.tensor.transpose(bank[0][:, h * P:h * P + rows], fl[0:rows, h, 0:P], ident[0:rows, 0:rows])
                    m = nc.tensor.transpose(bank[1][:, h * P:h * P + rows], fl[0:rows, h, P:2 * P],
                                            ident[0:rows, 0:rows])
                m.then_inc(turned, 1)

                def count(t, known):
                    pe.wait_ge(hot_made, 2 * t.n + 2)
                    m = nc.tensor.matmul(bank[2][:, 0:NT], oh_lo[t.u][:, :], oh_hi[t.u][:, 0:NT],
                                         start=(known == 0), stop=(known == NC - 1), skip_group_check=True)
                    m.then_inc(hot_used, 1)
                    if known == NC - 1:
                        pe.wait_ge(hot_used, NC)
                        nc.tensor.transpose(bank[7][0:P, 0:P], ident[:, :], ident[:, :]).then_inc(counted, 1)
                run_tiles(pe, NC, 4, count)
                pe.wait_ge(counted, 2)
                for h, rows in THALF:
                    m = nc.tensor.matmul(bank[3][0:rows, h:h + 1], deg[:, h * P:h * P + rows], ones[:, 0:1],
                                         start=True, stop=True, skip_group_check=True)
                m.then_inc(turned, 1)
                pe.wait_ge(turned, 4)
                for h, _ in THALF:
                    m = nc.tensor.matmul(bank[4][:, h:h + 1], before[:, :], cnt[:, h:h + 1], start=True, stop=(h == 0),
                                         skip_group_check=True)
                    if h:
                        m = nc.tensor.matmul(bank[4][:, h:h + 1], ones[:, :], cnt[:, 0:1], start=False, stop=True,
                                             skip_group_check=True)
                m.then_inc(counted, 1)
                pe.wait_ge(turned, 5)
                nc.tensor.matmul(bank[5][:, 0:1], ones[:, :], ok[:, 0:1], start=True, stop=True).then_inc(turned, 1)
                for after_step in (7, 9):
                    pe.wait_ge(turned, after_step)
                    for k in range(CHUNKS):
                        for h, rows in THALF:
                            m = nc.tensor.transpose(bank[6 + k][:, h * P:h * P + rows],
                                                    fl2[0:rows, h, k * P:(k + 1) * P], ident[0:rows, 0:rows])
                    m.then_inc(turned, 1)

        x_in = [sem(f"x_in{u}") for u in range(NORM_SLOTS)]
        h_out = [sem(f"h_out{u}") for u in range(NORM_SLOTS)]
        st_made, ag_made, ve_made, rs_made = sem("n_stats"), sem("n_mean_var"), sem("n_var_eps"), sem("n_rstd")
        sc_made, co_made, hn_made = sem("n_scale"), sem("n_coefs"), sem("n_h")
        NX = [*Self, *Xt]
        NH = [*Cv, *Y]

        def rows_of(known):
            return LAST if known == NT - 1 else P

        with nc.Block() as block:
            @block.sync
            def _(sp):
                def load(t, known):
                    r = rows_of(known)
                    if known is None or known >= NORM_SLOTS:
                        sp.wait_ge(hn_made, t.n - NORM_SLOTS + 1)
                    sp.dma_start(NX[t.u][0:r, :], x[bass.ds(t.n * P, r), :]).then_inc(x_in[t.u], 16)
                run_tiles(sp, NT, NORM_SLOTS, load)
                for u in range(NORM_SLOTS):
                    sp.wait_ge(x_in[u], 16 * len(range(u, NT, NORM_SLOTS)))

            @block.vector
            def _(dve):
                def keep(t):
                    m = small[t.u]
                    nc.vector.tensor_copy(rstd_x[:, bass.ds(t.n, 1)], m[:, 9:10])
                    nc.vector.scalar_tensor_tensor(nb_x[:, bass.ds(t.n, 1)], m[:, 6:7], -1.0, m[:, 9:10],
                                                   ALU.mult, ALU.mult)

                def coefs(t):
                    m = small[t.u]
                    nc.vector.tensor_tensor(m[:, 10:11], m[:, 9:10], dinv[:, bass.ds(t.n, 1)], ALU.mult)\
                        .then_inc(sc_made, 1)
                    dve.wait_ge(sc_made, t.n + 1)
                    nc.vector.scalar_tensor_tensor(m[:, 11:12], m[:, 6:7], -1.0, m[:, 10:11], ALU.mult, ALU.mult)\
                        .then_inc(co_made, 1)

                def stats(t, known):
                    m = small[t.u]
                    dve.wait_ge(x_in[t.u], 16 * (t.i + 1))
                    if known is None or known >= NORM_SLOTS:
                        dve.wait_ge(hn_made, t.n - NORM_SLOTS + 1)
                    nc.vector.bn_stats(m[:, 0:6], NX[t.u][:, :]).then_inc(st_made, 1)
                    if known != 0:
                        dve.wait_ge(rs_made, t.n)
                        dve.wait_ge(st_made, t.n + 1)
                        keep(t.after(-1))
                    else:
                        dve.wait_ge(st_made, 1)
                    nc.vector.bn_aggr(m[:, 6:8], m[:, 0:6]).then_inc(ag_made, 1)
                    if known != 0:
                        coefs(t.after(-1))
                    dve.wait_ge(ag_made, t.n + 1)
                    nc.vector.tensor_scalar(m[:, 8:9], m[:, 7:8], EPS, None, ALU.add).then_inc(ve_made, 1)
                    if known == NT - 1:
                        dve.wait_ge(rs_made, NT)
                        keep(t)
                        coefs(t)
                run_tiles(dve, NT, NORM_SLOTS, stats)

            @block.gpsimd
            def _(pool):
                def power(t, known):
                    m = small[t.u]
                    pool.wait_ge(ve_made, t.n + 1)
                    nc.gpsimd.tensor_tensor(m[:, 9:10], m[:, 8:9], neg_half[:, 0:1], ALU.pow).then_inc(rs_made, 1)
                run_tiles(pool, NT, NORM_SLOTS, power)

            @block.scalar
            def _(act):
                def store(t, known):
                    r = rows_of(known)
                    act.wait_ge(hn_made, t.n + 1)
                    act.dma_start(H[0][bass.ds(t.n * P, r), :], NH[t.u][0:r, :]).then_inc(h_out[t.u], 16)

                def normalise(t, known):
                    m = small[t.u]
                    act.wait_ge(co_made, t.n + 1)
                    if known is None or known >= NORM_SLOTS:
                        act.wait_ge(h_out[t.u], 16 * t.i)
                    nc.scalar.activation(NH[t.u][:, :], NX[t.u][:, :], ACT.Relu, bias=m[:, 11:12],
                                         scale=m[:, 10:11]).then_inc(hn_made, 1)
                    if known != 0:
                        store(t.after(-1), None)
                    if known == NT - 1:
                        store(t, known)
                run_tiles(act, NT, NORM_SLOTS, normalise)
                for u in range(NORM_SLOTS):
                    act.wait_ge(h_out[u], 16 * len(range(u, NT, NORM_SLOTS)))

        g_copied, g_idx, g_rows, g_add = sem("g_copied"), sem("g_indices"), sem("g_rows"), sem("g_added")
        g_step, g_sum, g_to = sem("g_step"), sem("g_summed"), sem("g_targets")
        gather_go, aggr_go = sem("gather_go"), sem("aggr_go")

        def general_sums(q):
            def k(c):
                return q * NC + c

            row_dst, M, Gs, Sum = Cv[0][:, 0:P], Cv[1], Y[0], Y[1]
            row_i32 = ints[:, 0, 0:P]
            def general_sync(sp):
                sp.dma_start(H[q][ROWS:ROWS + (NT - 1) * P, :], H[q][0:(NT - 1) * P, :]).then_inc(g_copied, 16)
                sp.dma_start(H[q][ROWS + (NT - 1) * P:ROWS + N, :], H[q][(NT - 1) * P:N, :]).then_inc(g_copied, 16)
                for z in range(2):
                    sp.dma_start(H[q][ROWS + NP + z * P:ROWS + NP + (z + 1) * P, :], G[0][:, 0, :])\
                        .then_inc(g_copied, 16)
                sp.wait_ge(g_copied, 64 * (q + 1))

                def fetch(c):
                    sp.dma_start(ints2[:, 0, 0:1], SRC[bass.ds(c * P, P), :]).then_inc(g_idx, 16)
                    sp.dma_start(ints2[:, 0, 1:2], DST[bass.ds(c * P, P), :]).then_inc(g_idx, 16)
                    sp.dma_start(row_i32, DST[bass.ds(c * P, P), :].rearrange("j o -> o j").broadcast_to([P, P]))\
                        .then_inc(g_idx, 16)

                fetch(0)
                with sp.Fori(1, NC) as c:
                    sp.wait_ge(g_add, 16 * k(c))
                    fetch(c)
                sp.wait_ge(g_add, 16 * k(NC))

            def general_pool(pool):
                last_row, last_sum = pool.to_reg(N - 1), pool.to_reg(2 * ROWS - 1)
                pool.wait_ge(g_copied, 64 * (q + 1))
                with pool.Fori(0, NC) as c:
                    pool.wait_ge(g_idx, 48 * (k(c) + 1))
                    pool.sem_inc(gather_go, 1)
                    pool.indirect_dma_start(Gs[:, :], None, H[q][0:N, :],
                                            bass.IndirectOffsetOnAxis(ap=ints2[:, 0, 0:1], axis=0),
                                            bounds_check=last_row, oob_is_err=False).then_inc(g_rows, 16)
                    pool.wait_ge(g_to, k(c) + 1)
                    pool.sem_inc(gather_go, 1)
                    pool.indirect_dma_start(H[q], bass.IndirectOffsetOnAxis(ap=ints2[:, 1, 0:1], axis=0),
                                            Sum[:, :], None, bounds_check=last_sum,
                                            compute_op=ALU.add).then_inc(g_add, 16)
                pool.wait_ge(g_add, 16 * k(NC))

            def general_vector(dve):
                with dve.Fori(0, NC) as c:
                    s = 7 * k(c)
                    dve.wait_ge(g_idx, 48 * (k(c) + 1))
                    nc.vector.tensor_copy(row_dst, row_i32)
                    nc.vector.tensor_copy(M[:, 2 * P:2 * P + 1], ints2[:, 0, 1:2]).then_inc(g_step, 1)
                    dve.wait_ge(g_step, s + 1)
                    nc.vector.tensor_scalar(M[:, 0:P], row_dst, M[:, 2 * P:2 * P + 1], None, ALU.is_equal)\
                        .then_inc(g_step, 1)
                    dve.wait_ge(g_step, s + 2)
                    nc.vector.tensor_tensor(M[:, P:2 * P], M[:, 0:P], after[:, :], ALU.mult).then_inc(g_step, 1)
                    dve.wait_ge(g_step, s + 3)
                    nc.vector.reduce_sum(M[:, 2 * P + 1:2 * P + 2], M[:, P:2 * P], mybir.AxisListType.X)\
                        .then_inc(g_step, 1)
                    dve.wait_ge(g_step, s + 4)
                    nc.vector.tensor_scalar(M[:, 2 * P + 2:2 * P + 3], M[:, 2 * P + 1:2 * P + 2], 0.0, None,
                                            ALU.is_equal)
                    nc.vector.tensor_scalar(M[:, 2 * P + 3:2 * P + 4], row[:, 0:1], -1.0, -float(TRASH),
                                            ALU.mult, ALU.add).then_inc(g_step, 1)
                    dve.wait_ge(g_step, s + 5)
                    nc.vector.tensor_tensor(M[:, 2 * P + 4:2 * P + 5], M[:, 2 * P:2 * P + 1],
                                            M[:, 2 * P + 3:2 * P + 4], ALU.add).then_inc(g_step, 1)
                    dve.wait_ge(g_step, s + 6)
                    nc.vector.scalar_tensor_tensor(M[:, 2 * P + 5:2 * P + 6], M[:, 2 * P + 4:2 * P + 5],
                                                   M[:, 2 * P + 2:2 * P + 3], M[:, 2 * P + 3:2 * P + 4],
                                                   ALU.mult, ALU.subtract).then_inc(g_step, 1)
                    dve.wait_ge(g_step, s + 7)
                    nc.vector.tensor_scalar(ints2[:, 1, 0:1], M[:, 2 * P + 5:2 * P + 6], float(ROWS), None,
                                            ALU.add)
                    dve.wait_ge(g_sum, k(c) + 1)
                    nc.vector.tensor_copy(Sum[:, :], bank[6][:, :]).then_inc(g_to, 1)
                dve.wait_ge(g_add, 16 * k(NC))

            def general_tensor(pe):
                with pe.Fori(0, NC) as c:
                    pe.wait_ge(g_rows, 16 * (k(c) + 1))
                    pe.wait_ge(g_step, 7 * k(c) + 2)
                    nc.tensor.matmul(bank[6][:, :], M[:, 0:P], Gs[:, :], start=True, stop=True)\
                        .then_inc(g_sum, 1)

            return general_sync, general_pool, general_vector, general_tensor

        names = dict(
            self_in=[sem(f"self_in{u}") for u in range(SLOTS)],
            edge_in=[sem(f"edge_in{u}") for u in range(SLOTS)],
            xt_in=[sem(f"xt_in{u}") for u in range(SLOTS)],
            ho_out=[sem(f"ho_out{u}") for u in range(SLOTS)],
            xo_out=[sem(f"xo_out{u}") for u in range(SLOTS)],
        )
        self_in, edge_in, xt_in, ho_out, xo_out = names.values()
        idx_made = sem("idx_made")
        s_made = sem("s_made")
        agg_done, hi_done, lo_done, main_done = sem("agg_done"), sem("hi_done"), sem("lo_done"), sem("main_done")
        conv_done, stats_done, mv_done, ve_done = sem("conv_done"), sem("stats_done"), sem("mv_done"), sem("ve_done")
        rstd_done, cg_done, y_done, gelu_done = sem("rstd_done"), sem("cg_done"), sem("y_done"), sem("gelu_done")
        h_done, r_done, rb_done = sem("h_done"), sem("r_done"), sem("rb_done")
        x2_done, st2_done, mv2_done, ve2_done = sem("x2_done"), sem("st2_done"), sem("mv2_done"), sem("ve2_done")
        rs2_done, sc2_done, co2_done, xb_done, res_done = (sem("rs2_done"), sem("sc2_done"), sem("co2_done"),
                                                           sem("xb_done"), sem("res_done"))

        def convolution(q):
            first, second, third = q == 0, q == 1, q == 2

            def uses(t, a_phase=q):
                return a_phase * len(range(t.u, NT, SLOTS)) + t.i + 1

            def upto(t, phase=q):
                return phase * NT + t.n + 1

            def wait_free(engine, s, t, known, phase=q):
                if known is not None and known < SLOTS:
                    if phase:
                        engine.wait_ge(s, phase * NT)
                else:
                    engine.wait_ge(s, phase * NT + t.n - SLOTS + 1)

            def shifted(known, k):
                return None if known is None else known + k

            general_sync, general_pool, general_vector, general_tensor = general_sums(q)

            def if_general(engine, program):
                flag = engine.value_load(general[0:1, 0:1], min_val=0, max_val=1)
                with engine.If(flag > 0):
                    program(engine)
                return flag

            with nc.Block() as block:
                @block.sync
                def _(sp):
                    general_reg = if_general(sp, general_sync)

                    def load_self(t, known):
                        r = rows_of(known)
                        wait_free(sp, agg_done, t, known)
                        sp.dma_start(Self[t.u][0:r, :], H[q][bass.ds(general_reg * ROWS + t.n * P, r), :])\
                            .then_inc(self_in[t.u], 16)

                    def load_x(t, known):
                        r = rows_of(known)
                        if second:
                            wait_free(sp, x2_done, t, known, 0)
                            sp.dma_start(Xt[t.u][0:r, :], x[bass.ds(t.n * P, r), :]).then_inc(xt_in[t.u], 16)
                        if third:
                            wait_free(sp, xb_done, t, known, 0)
                            sp.dma_start(Xt[t.u][0:r, :], X2[bass.ds(t.n * P, r), :]).then_inc(xt_in[t.u], 16)

                    def store(t, known):
                        r = rows_of(known)
                        if first:
                            sp.wait_ge(h_done, upto(t))
                            sp.dma_start(H[1][bass.ds(t.n * P, r), :], Ho[t.u][0:r, :]).then_inc(ho_out[t.u], 16)
                        if second:
                            sp.wait_ge(x2_done, upto(t, 0))
                            sp.dma_start(X2[bass.ds(t.n * P, r), :], X2t[t.u][0:r, :]).then_inc(xo_out[t.u], 16)
                            sp.wait_ge(h_done, upto(t))
                            sp.dma_start(H[2][bass.ds(t.n * P, r), :], Ho[t.u][0:r, :]).then_inc(ho_out[t.u], 16)
                        if third:
                            sp.wait_ge(res_done, upto(t, 0))
                            sp.dma_start(out[bass.ds(t.n * P, r), :], Cv[t.u][0:r, :]).then_inc(xo_out[t.u], 16)

                    def body(t, known):
                        if known == 0:
                            for k in range(3):
                                load_self(t.after(k), k)
                            for k in range(2):
                                load_x(t.after(k), k)
                        if known is None or known + 3 < NT:
                            load_self(t.after(3), shifted(known, 3))
                        if known is None or known + 2 < NT:
                            load_x(t.after(2), shifted(known, 2))
                        if known != 0:
                            store(t.after(-1), shifted(known, -1))
                        if known == NT - 1:
                            store(t, known)
                    run_tiles(sp, NT, SLOTS, body)
                    for u in range(SLOTS):
                        n = len(range(u, NT, SLOTS))
                        if not third:
                            sp.wait_ge(ho_out[u], 16 * (q + 1) * n)
                        if not first:
                            sp.wait_ge(xo_out[u], 16 * q * n)

                @block.gpsimd
                def _(pool):
                    if_general(pool, general_pool)

                    def indices(t, known):
                        if known is None or known >= SLOTS:
                            pool.wait_ge(edge_in[t.u], 16 * CHUNKS * (uses(t) - 1))
                        nc.gpsimd.tensor_copy(idx[t.u][:, :], edge_from[:, :, bass.ds(t.n, 1)]
                                              .rearrange("p k o -> p (k o)")).then_inc(idx_made, 1)

                    def gather_free(t, known):
                        wait_free(pool, agg_done, t, known)
                        pool.wait_ge(idx_made, upto(t))
                        pool.sem_inc(gather_go, 1)

                    def fetch(t):
                        for k in range(CHUNKS):
                            pool.indirect_dma_start(G[t.u][:, k, :], None, H[q][0:N, :],
                                                    bass.IndirectOffsetOnAxis(ap=idx[t.u][:, k:k + 1], axis=0),
                                                    bounds_check=N - 1, oob_is_err=False).then_inc(edge_in[t.u], 16)

                    def residual(t, known):
                        if second:
                            pool.wait_ge(r_done, upto(t, 0))
                            nc.gpsimd.tensor_tensor(R[t.u][:, :], R[t.u][:, :], beta_b[1][:, :], ALU.add)\
                                .then_inc(rb_done, 1)
                        if third:
                            pool.wait_ge(xt_in[t.u], 16 * (uses(t, 1)))
                            wait_free(pool, res_done, t, known, 0)
                            nc.gpsimd.tensor_tensor(R[t.u][:, :], Xt[t.u][:, :], bias_b[2][:, :], ALU.add)\
                                .then_inc(xb_done, 1)

                    def body(t, known):
                        if known == 0:
                            for k in range(3):
                                indices(t.after(k), k)
                                gather_free(t.after(k), k)
                                fetch(t.after(k))
                            residual(t, 0)
                        has3 = known is None or known + 3 < NT
                        if has3:
                            indices(t.after(3), shifted(known, 3))
                            gather_free(t.after(3), shifted(known, 3))
                            fetch(t.after(3))
                        if third and known != NT - 1:
                            residual(t.after(1), shifted(known, 1))
                        if not third:
                            m = small[t.u]
                            late = second and known != 0
                            c = slice(8, 25, 16) if late else slice(8, 9)
                            d = slice(9, 26, 16) if late else slice(9, 10)
                            pool.wait_ge(ve_done, upto(t))
                            nc.gpsimd.tensor_tensor(m[:, d], m[:, c], neg_half[:, 0:1 + late], ALU.pow)\
                                .then_inc(rstd_done, 1)
                        if second and known != NT - 1:
                            residual(t.after(1), shifted(known, 1))
                        elif second:
                            m = small[t.after(1).u]
                            pool.wait_ge(ve_done, upto(t) + 1)
                            nc.gpsimd.tensor_tensor(m[:, 25:26], m[:, 24:25], neg_half[:, 0:1], ALU.pow)\
                                .then_inc(rstd_done, 1)
                    run_tiles(pool, NT, SLOTS, body)

                @block.scalar
                def _(act):
                    def high(t):
                        act.wait_ge(agg_done, upto(t))
                        nc.scalar.activation(Ahi[t.u][:, :], Agg[t.u][:, :], ACT.Copy).then_inc(hi_done, 1)

                    def relu_x(t, known):
                        act.wait_ge(xt_in[t.u], 16 * uses(t, 0))
                        wait_free(act, y_done, t, known)
                        nc.scalar.activation(R[t.u][:, :], Xt[t.u][:, :], ACT.Relu, bias=nb_x[:, bass.ds(t.n, 1)],
                                             scale=rstd_x[:, bass.ds(t.n, 1)]).then_inc(r_done, 1)

                    def relu_x2(t, known):
                        m = small[t.after(1).u]
                        act.wait_ge(co2_done, upto(t, 0))
                        if known is None or known >= SLOTS:
                            act.wait_ge(ho_out[t.u], 16 * (uses(t) - 1))
                        nc.scalar.activation(Ho[t.u][:, :], X2t[t.u][:, :], ACT.Relu, bias=m[:, 27:28],
                                             scale=m[:, 26:27]).then_inc(h_done, 1)

                    def body(t, known):
                        if known == 0:
                            high(t)
                            high(t.after(1))
                            if second:
                                relu_x(t, 0)
                        if known is None or known + 2 < NT:
                            high(t.after(2))
                        if second and known != NT - 1:
                            relu_x(t.after(1), shifted(known, 1))
                        if second and known != 0:
                            relu_x2(t.after(-1), shifted(known, -1))
                        if not third:
                            act.wait_ge(y_done, upto(t))
                            nc.scalar.activation(Y[t.u][:, :], Y[t.u][:, :], ACT.Gelu).then_inc(gelu_done, 1)
                        if first:
                            if known is None or known >= SLOTS:
                                act.wait_ge(ho_out[t.u], 16 * (uses(t) - 1))
                            act.wait_ge(gelu_done, upto(t))
                            nc.scalar.activation(Ho[t.u][:, :], Y[t.u][:, :], ACT.Copy,
                                                 scale=dinv[:, bass.ds(t.n, 1)]).then_inc(h_done, 1)
                        if second and known == NT - 1:
                            relu_x2(t, known)
                    run_tiles(act, NT, SLOTS, body)

                @block.vector
                def _(dve):
                    if_general(dve, general_vector)

                    def select(t):
                        for k in range(CHUNKS):
                            i = nc.vector.tensor_scalar(S[t.u][:, k, :], col[:, 0:P], edge_to[:, k, bass.ds(t.n, 1)],
                                                        None, ALU.is_equal)
                        i.then_inc(s_made, 1)

                    def low(t):
                        dve.wait_ge(hi_done, upto(t))
                        nc.vector.tensor_tensor(Alo[t.u][:, :], Agg[t.u][:, :], Ahi[t.u][:, :].bitcast(F32),
                                                ALU.subtract).then_inc(lo_done, 1)

                    def x2_sum(t, known):
                        dve.wait_ge(gelu_done, upto(t))
                        if known is None or known >= SLOTS:
                            dve.wait_ge(xo_out[t.u], 16 * (uses(t, 0) - 1))
                            dve.wait_ge(h_done, upto(t) - SLOTS)
                        nc.vector.tensor_tensor(X2t[t.u][:, :], Xt[t.u][:, :], Y[t.u][:, :], ALU.add)\
                            .then_inc(x2_done, 1)

                    def x2_stats(t):
                        m = small[t.after(1).u]
                        dve.wait_ge(x2_done, upto(t, 0))
                        nc.vector.bn_stats(m[:, 16:22], X2t[t.u][:, :]).then_inc(st2_done, 1)

                    def x2_coefs(t):
                        m = small[t.after(1).u]
                        nc.vector.tensor_tensor(m[:, 26:27], m[:, 25:26], dinv[:, bass.ds(t.n, 1)], ALU.mult)\
                            .then_inc(sc2_done, 1)
                        dve.wait_ge(sc2_done, upto(t, 0))
                        nc.vector.scalar_tensor_tensor(m[:, 27:28], m[:, 22:23], -1.0, m[:, 26:27], ALU.mult, ALU.mult)\
                            .then_inc(co2_done, 1)

                    def select_next(t, known):
                        wait_free(dve, agg_done, t.after(3), shifted(known, 3))
                        select(t.after(3))

                    def var_eps(t, late):
                        m = small[t.u]
                        c = slice(7, 24, 16) if late else slice(7, 8)
                        d = slice(8, 25, 16) if late else slice(8, 9)
                        dve.wait_ge(mv_done, upto(t))
                        nc.vector.tensor_scalar(m[:, d], m[:, c], EPS, None, ALU.add).then_inc(ve_done, 1)

                    def body(t, known):
                        m = small[t.u]
                        late = second and known != 0
                        prev = t.after(-1)
                        has2, has3 = (known is None or known + k < NT for k in (2, 3))
                        if known == 0:
                            for k in range(3):
                                wait_free(dve, agg_done, t.after(k), k)
                                select(t.after(k))
                            low(t)
                            low(t.after(1))
                        dve.wait_ge(main_done, upto(t))
                        if third:
                            dve.wait_ge(xb_done, upto(t, 0))
                            if known is None or known >= SLOTS:
                                dve.wait_ge(xo_out[t.u], 16 * (uses(t, 1) - 1))
                            nc.vector.scalar_tensor_tensor(Cv[t.u][:, :], Out[t.u][:, :], dinv[:, bass.ds(t.n, 1)],
                                                           R[t.u][:, :], ALU.mult, ALU.add).then_inc(res_done, 1)
                            if has3:
                                select_next(t, known)
                            if has2:
                                low(t.after(2))
                            return
                        nc.vector.scalar_tensor_tensor(Cv[t.u][:, :], Out[t.u][:, :], dinv[:, bass.ds(t.n, 1)],
                                                       bias_b[q][:, :], ALU.mult, ALU.add).then_inc(conv_done, 1)
                        dve.wait_ge(conv_done, upto(t))
                        nc.vector.bn_stats(m[:, 0:6], Cv[t.u][:, :]).then_inc(stats_done, 1)
                        if late:
                            x2_sum(prev, shifted(known, -1))
                        elif has3:
                            select_next(t, known)
                        dve.wait_ge(stats_done, upto(t))
                        dve.sem_inc(aggr_go, 1)
                        nc.vector.bn_aggr(m[:, 6:8], m[:, 0:6]).then_inc(mv_done, 1)
                        if late:
                            x2_stats(prev)
                        else:
                            var_eps(t, late)
                        dve.wait_ge(mv_done, upto(t))
                        nc.vector.scalar_tensor_tensor(Cv[t.u][:, :], Cv[t.u][:, :], m[:, 6:7], gamma_b[q][:, :],
                                                       ALU.subtract, ALU.mult).then_inc(cg_done, 1)
                        if late:
                            dve.wait_ge(st2_done, upto(prev, 0))
                            dve.sem_inc(aggr_go, 1)
                            nc.vector.bn_aggr(m[:, 22:24], m[:, 16:22]).then_inc(mv2_done, 1)
                            dve.wait_ge(mv2_done, upto(prev, 0))
                            var_eps(t, late)
                        if has2:
                            low(t.after(2))
                        if late:
                            if has3:
                                select_next(t, known)
                            dve.wait_ge(rstd_done, upto(t))
                            x2_coefs(prev)
                        else:
                            dve.wait_ge(rstd_done, upto(t))
                        dve.wait_ge(cg_done, upto(t))
                        if first:
                            wait_free(dve, h_done, t, known)
                            plus = beta_b[0]
                        else:
                            dve.wait_ge(rb_done, upto(t, 0))
                            plus = R[t.u]
                        nc.vector.scalar_tensor_tensor(Y[t.u][:, :], Cv[t.u][:, :], m[:, 9:10], plus[:, :],
                                                       ALU.mult, ALU.add).then_inc(y_done, 1)
                        if second and known == NT - 1:
                            m = small[t.after(1).u]
                            x2_sum(t, known)
                            x2_stats(t)
                            dve.wait_ge(st2_done, NT)
                            nc.vector.bn_aggr(m[:, 22:24], m[:, 16:22]).then_inc(mv2_done, 1)
                            dve.wait_ge(mv2_done, NT)
                            nc.vector.tensor_scalar(m[:, 24:25], m[:, 23:24], EPS, None, ALU.add).then_inc(ve_done, 1)
                            dve.wait_ge(rstd_done, upto(t) + 1)
                            x2_coefs(t)
                    run_tiles(dve, NT, SLOTS, body)

                @block.tensor
                def _(pe):
                    if_general(pe, general_tensor)

                    def aggregate(t, known):
                        pe.wait_ge(self_in[t.u], 16 * uses(t))
                        pe.wait_ge(edge_in[t.u], 16 * CHUNKS * uses(t))
                        pe.wait_ge(s_made, upto(t))
                        for f in range(KD):
                            fs = slice(f * P, (f + 1) * P)
                            nc.tensor.matmul(Agg[t.u][:, fs], Self[t.u][:, fs], ident[:, :], is_transpose=True,
                                             start=True, stop=False, skip_group_check=True)
                            for k in range(CHUNKS):
                                m = nc.tensor.matmul(Agg[t.u][:, fs], G[t.u][:, k, fs], S[t.u][:, k, :],
                                                     start=False, stop=(k == CHUNKS - 1), skip_group_check=True)
                        m.then_inc(agg_done, 1)

                    def multiply(t, known):
                        pe.wait_ge(hi_done, upto(t))
                        if not third:
                            wait_free(pe, conv_done, t, known)
                        else:
                            if known is not None and known < SLOTS:
                                pe.wait_ge(conv_done, 2 * NT)
                            else:
                                pe.wait_ge(res_done, t.n - SLOTS + 1)
                        n = 0
                        for a, w in ((Ahi, Whi), (Ahi, Wlo), (Alo, Whi)):
                            if a is Alo:
                                pe.wait_ge(lo_done, upto(t))
                            for f in range(KD):
                                m = nc.tensor.matmul(Out[t.u][:, :], a[t.u][:, f * P:(f + 1) * P], w[q][:, f, :],
                                                     start=(n == 0), stop=(n == 3 * KD - 1))
                                n += 1
                        m.then_inc(main_done, 1)

                    def body(t, known):
                        if known == 0:
                            aggregate(t, 0)
                        if known != NT - 1:
                            aggregate(t.after(1), shifted(known, 1))
                        multiply(t, known)
                    run_tiles(pe, NT, SLOTS, body)

        for q in range(3):
            convolution(q)


_INS = ['x', 'src', 'dst', 'L0_gnn_W1', 'L0_gnn_b1', 'L0_gnn_gamma1', 'L0_gnn_beta1', 'L0_gnn_W2', 'L0_gnn_b2',
        'L0_gnn_gamma2', 'L0_gnn_beta2', 'L1_gnn_W', 'L1_gnn_b']


def kernel(**inputs):
    import numpy as _np
    import concourse.bacc as _bacc
    from concourse import mybir as _mybir
    from concourse.bass_utils import run_bass_kernel_spmd as _run

    nc = _bacc.Bacc("TRN2", target_bir_lowering=False, num_devices=1)
    arrays, args = {}, []
    for name in _INS:
        a = _np.ascontiguousarray(inputs[name])
        arrays[f"in_{name}_dram"] = a
        args.append(nc.dram_tensor(f"in_{name}_dram", a.shape, _mybir.dt.from_np(a.dtype), kind="ExternalInput").ap())
    out = nc.dram_tensor("out_0_dram", inputs["x"].shape, _mybir.dt.float32, kind="ExternalOutput").ap()
    gnn_kernel(nc, *args, out)
    r = _run(nc, [arrays], core_ids=[0])
    return r.results[0]["out_0_dram"]
```

```python
from contextlib import ExitStack

import concourse.bass as bass
from concourse import mybir

P = 128
ALU = mybir.AluOpType
ACT = mybir.ActivationFunctionType
F32 = mybir.dt.float32
F32R = mybir.dt.float32r
BF16 = mybir.dt.bfloat16
I32 = mybir.dt.int32

EPS = 1e-5
PAIRS = 2
SLOTS = 2 * PAIRS
CHUNKS = 3
WINDOW = 2 * P
OVER = P // 2
NOWHERE = 1 << 16


class Tile:

    def __init__(self, i, u, slots):
        self.i, self.u, self.slots = i, u, slots

    @property
    def n(self):
        return self.i * self.slots + self.u

    def after(self, k):
        return Tile(self.i + (self.u + k) // self.slots, (self.u + k) % self.slots, self.slots)


def run_tiles(engine, count, slots, body, ahead=2):
    last = max((count - ahead) // slots, 1)
    for n in range(slots):
        body(Tile(0, n, slots), n)
    if last > 1:
        with engine.Fori(1, last) as i:
            for u in range(slots):
                body(Tile(i, u, slots), None)
    for n in range(last * slots, count):
        body(Tile(n // slots, n % slots, slots), n)


def gnn_kernel(nc, x, src, dst, W1, b1, g1, be1, W2, b2, g2, be2, W3, b3, out):
    N, D = x.shape
    E = src.shape[0]
    NT = -(-N // P)
    NPAIR = -(-NT // 2)
    NTE = 2 * NPAIR
    NP = NT * P
    LAST = N - (NT - 1) * P
    NC = -(-E // P)
    EL = E - (NC - 1) * P
    KD = D // P
    THALF = [(h, min(P, NTE - h * P)) for h in range(-(-NTE // P))]
    CHALF = [(h, min(P, NC - h * P)) for h in range(-(-NC // P))]
    TRASH = NP + P
    ROWS = NP + 2 * P
    assert D == 512 and NT <= 2 * P and NC <= 2 * P and NTE > 3 * SLOTS and NT % 2

    with ExitStack() as ctx:
        def sb(name, shape, dt=F32):
            return ctx.enter_context(nc.sbuf_tensor(name, shape, dt))

        def sem(name):
            return ctx.enter_context(nc.semaphore(name))

        def scratch(name, shape, dt=F32):
            return nc.dram_tensor(name, shape, dt, kind="Internal").ap()

        H = [scratch(f"H{q}", (2 * ROWS, D)) for q in range(3)]
        X2 = scratch("X2", (NP, D))
        SRC = scratch("src_padded", (E + 2 * WINDOW, 1), I32)
        DST = scratch("dst_padded", (E + 2 * WINDOW, 1), I32)

        COEF = scratch("coefficients", (NTE * P, 2))

        ident = sb("ident", [P, P])
        ones = sb("ones", [P, P])
        before = sb("before", [P, P])
        after = sb("after", [P, P])
        col_i = sb("col_i", [P, 2 * P], I32)
        row_i = sb("row_i", [P, 1], I32)
        col = sb("col", [P, 2 * P])
        colb = sb("colb", [P, 2 * P], BF16)
        row = sb("row", [P, 3])
        neg_half = sb("neg_half", [P, 2 * P])
        dinv = sb("dinv", [P, NTE])
        deg1 = sb("deg1", [P, NTE])
        eps2 = sb("eps2", [P, NTE])
        sq_hi = sb("sq_hi", [P, 2, 3, P], F32R)
        B3 = [sb(f"B3_{q}", [3, D], F32R) for q in range(2)]
        SQ = scratch("SQ", (NTE, 3 * P))
        edge_to = sb("edge_to", [P, NTE])
        over_to = sb("over_to", [P, NPAIR])
        edge_from = sb("edge_from", [P, CHUNKS, NPAIR], I32)
        col_win = sb("col_win", [P, WINDOW])
        odd = sb("odd", [P, 4])
        mv_x = sb("mv_x", [P, NTE, 2])
        rstd_x, nb_x = sb("rstd_x", [P, NTE]), sb("nb_x", [P, NTE])
        scale_h, off_h = sb("scale_h", [P, NTE]), sb("off_h", [P, NTE])
        edge_co = [sb(f"edge_co{u}", [P, CHUNKS, 2]) for u in range(PAIRS)]
        general = sb("general", [P, 1], I32)
        Whi = [sb(f"Whi{q}", [P, KD, D], F32R) for q in range(3)]
        Wlo = [sb(f"Wlo{q}", [P, KD, D], F32R) for q in range(3)]
        vecs = [sb(f"vec{k}", [P, D]) for k in range(7)]
        bias_b, gamma_b, beta_b = vecs[0:3], vecs[3:5], vecs[5:7]

        SelfP = [sb(f"self{u}", [P, 2, D]) for u in range(PAIRS)]
        G = [sb(f"g{u}", [P, CHUNKS, D]) for u in range(PAIRS)]
        S = [sb(f"s{u}", [P, 2, P]) for u in range(PAIRS)]
        Sv = [sb(f"sv{u}", [P, 2 * P], F32R) for u in range(PAIRS)]
        Vhi = [sb(f"vhi{u}", [P, D], F32R) for u in range(PAIRS)]
        Vlo = [sb(f"vlo{u}", [P, D], F32R) for u in range(PAIRS)]
        Ahi = [sb(f"ahi{u}", [P, KD * 2 * P], F32R) for u in range(PAIRS)]
        Alo = [sb(f"alo{u}", [P, KD * 2 * P], F32R) for u in range(PAIRS)]
        CvP, YP, XtP, RP, X2P, HoP = ([sb(f"{name}{u}", [P, 2, D]) for u in range(PAIRS)]
                                      for name in ("conv", "y", "x", "r", "x2", "ho"))
        idx = [sb(f"idx{u}", [P, CHUNKS], I32) for u in range(PAIRS)]
        root = [sb(f"root{u}", [3, 2, P], F32R) for u in range(PAIRS)]
        small = [sb(f"small{u}", [P, 32]) for u in range(SLOTS)]
        XH, RH, VH = XtP, RP, [pair[:, 0, :] for pair in X2P]
        Self, Cv, Y, Xt, R, X2t, Ho = ([pair[u][:, j, :] for u in range(PAIRS) for j in range(2)]
                                       for pair in (SelfP, CvP, YP, XtP, RP, X2P, HoP))

        Agg = [ctx.enter_context(nc.psum_tensor(f"agg{u}", [P, KD * 2 * P], F32)) for u in range(PAIRS)]
        Out = [ctx.enter_context(nc.psum_tensor(f"out{u}", [P, D], F32)) for u in range(SLOTS)]
        bank = [Agg[b // 2][:, b % 2 * D:(b % 2 + 1) * D] for b in range(2 * PAIRS)] + [o[:, :] for o in Out]

        ints = sb("ints", [P, 2, WINDOW], I32)
        ints2 = sb("ints2", [P, 2, WINDOW], I32)
        aggr_go = sem("aggr_go")
        fl, fl2 = (pair[:, :, 0:WINDOW] for pair in HoP)
        b_hi, b_lo = Ahi[0][0:3, 0:D], Cv[0][0:3, :]
        lo_t = sb("lo_t", [P, NC])
        hi_t = sb("hi_t", [P, NC])
        deg = sb("deg", [P, NTE])
        sq = sb("sq", [P, NTE])
        roots, roots_out = sem("roots"), sem("roots_out")
        oh_lo = [sb(f"oh_lo{u}", [P, P], BF16) for u in range(4)]
        oh_hi = [sb(f"oh_hi{u}", [P, 2 * P], BF16) for u in range(4)]
        cnt = sb("cnt", [P, 2])
        start_i = sb("start_i", [P, 2, 2], I32)
        seen = sb("seen", [P, 2])
        ok = sb("ok", [P, 2])
        pad_i = sb("pad_i", [2, WINDOW], I32)

        loaded = sem("edges_loaded")
        weights = sem("weights_loaded")
        vectors = sem("vectors_loaded")
        padded = sem("edges_padded")
        pads = sem("pads_written")
        consts = sem("consts_made")
        cols = sem("columns_made")
        dve1 = sem("dve_step")
        w_split = sem("weights_split")
        w_free = sem("weights_staged_free")
        turned = sem("edges_turned")
        hot_made = sem("one_hots_made")
        hot_used = sem("one_hots_used")
        counted = sem("degrees_counted")
        windows = sem("windows_fetched")

        nr_made = sem("newton_step")

        def newton(dve, y, d, spare, s, base):
            nc.vector.tensor_tensor(spare[:, :], y[:, :], y[:, :], ALU.mult).then_inc(s, 1)
            dve.wait_ge(s, base + 1)
            nc.vector.tensor_tensor(spare[:, :], spare[:, :], d[:, :], ALU.mult).then_inc(s, 1)
            dve.wait_ge(s, base + 2)
            nc.vector.tensor_scalar(spare[:, :], spare[:, :], -0.5, 1.5, ALU.mult, ALU.add).then_inc(s, 1)
            dve.wait_ge(s, base + 3)
            nc.vector.tensor_tensor(y[:, :], y[:, :], spare[:, :], ALU.mult).then_inc(s, 1)
            dve.wait_ge(s, base + 4)

        stage = Self

        with nc.Block() as block:
            @block.sync
            def _(sp):
                sp.wait_ge(consts, 1)
                for h, rows in CHALF:
                    full = rows if h < len(CHALF) - 1 or EL == P else rows - 1
                    sp.dma_start(ints[0:full, h, 0:P],
                                 dst[h * P * P:(h * P + full) * P].rearrange("(c j) -> c j", j=P)).then_inc(loaded, 16)
                    if full < rows:
                        sp.dma_start(ints[full:rows, h, 0:EL],
                                     dst[(NC - 1) * P:E].rearrange("(a j) -> a j", a=1)).then_inc(loaded, 16)
                for a, b in ((src, SRC), (dst, DST)):
                    r = next(k for k in (16, 15, 12, 10, 8, 6, 5, 4, 3, 2, 1) if E % k == 0)
                    sp.dma_start(b[0:E, :].rearrange("(a j) o -> a (j o)", a=r),
                                 a.rearrange("(a j) -> a j", a=r)).then_inc(padded, 16)
                sp.wait_ge(pads, 1)
                sp.dma_start(SRC[E:E + 2 * WINDOW, :].rearrange("(a j) o -> a (j o)", a=2), pad_i[:, :])\
                    .then_inc(padded, 16)
                sp.wait_ge(padded, 48)
                sp.wait_ge(pads, 2)
                sp.dma_start(DST[E:E + 2 * WINDOW, :].rearrange("(a j) o -> a (j o)", a=2), pad_i[:, :])\
                    .then_inc(padded, 16)
                for k, v in enumerate((b1, b2, b3, g1, g2, be1, be2)):
                    sp.dma_start(vecs[k][:, :], v.rearrange("(a d) -> a d", a=1).broadcast_to([P, D]))\
                        .then_inc(vectors, 16)
                for q, w in enumerate((W1, W2, W3)):
                    wv = w.rearrange("(k p) n -> k p n", p=P)
                    if q:
                        sp.wait_ge(w_free, 4 * q)
                    for k in range(KD):
                        sp.dma_start(stage[k][:, :], wv[k, :, :]).then_inc(weights, 16)
                sp.wait_ge(roots, 4)
                for h, rows in THALF:
                    sp.dma_start(SQ[h * P:h * P + rows, :], sq_hi[0:rows, h, :, :].bitcast(F32)
                                 .rearrange("p a j -> p (a j)")).then_inc(roots_out, 16)
                sp.wait_ge(roots_out, 16 * len(THALF))
                sp.wait_ge(vectors, 16 * 7)
                sp.wait_ge(weights, 16 * 3 * KD)
                sp.wait_ge(padded, 64)

            @block.gpsimd
            def _(pool):
                nc.gpsimd.memset(ints[:, :, :], -1).then_inc(consts, 1)
                nc.gpsimd.iota(col_i[:, :], pattern=[[1, 2 * P]], base=0, channel_multiplier=0).then_inc(cols, 1)
                nc.gpsimd.iota(row_i[:, :], pattern=[[0, 1]], base=0, channel_multiplier=1).then_inc(cols, 1)
                nc.gpsimd.memset(pad_i[:, :], 0).then_inc(pads, 1)
                pool.wait_ge(padded, 48)
                nc.gpsimd.memset(pad_i[:, :], NP).then_inc(pads, 1)
                pool.wait_ge(counted, 5)
                pool.wait_ge(padded, 64)
                for h, rows in THALF:
                    for a, o in ((SRC, ints2), (DST, ints)):
                        for k in range(2):
                            pool.indirect_dma_start(
                                o[0:rows, h, k * P:(k + 1) * P], None, a,
                                bass.IndirectOffsetOnAxis(ap=start_i[0:rows, k, h:h + 1], axis=0),
                                bounds_check=E + P, oob_is_err=False).then_inc(windows, 16)

            @block.scalar
            def _(act):
                act.wait_ge(roots, 1)
                nc.scalar.activation(dinv[:, :], sq[:, :], ACT.Sqrt).then_inc(counted, 1)
                for q in range(3):
                    for k in range(KD):
                        act.wait_ge(weights, 16 * KD * (q + 1))
                        nc.scalar.activation(Whi[q][:, k, :], stage[k][:, :], ACT.Copy).then_inc(w_split, 1)

            @block.vector
            def _(dve):
                n = [0]

                def link(ins):
                    n[0] += 1
                    ins.then_inc(dve1, 1)
                    dve.wait_ge(dve1, n[0])

                nc.vector.memset(ones[:, :], 1.0)
                nc.vector.memset(neg_half[:, :], -0.5)
                nc.vector.memset(mv_x[:, :, :], 0.0)
                for c in edge_co:
                    nc.vector.memset(c[:, :, :], 0.0)
                for g in G:
                    link(nc.vector.memset(g[:, :, :], 0.0))
                dve.wait_ge(cols, 2)
                nc.vector.tensor_copy(col[:, :], col_i[:, :])
                nc.vector.tensor_copy(colb[:, :], col_i[:, :])
                link(nc.vector.tensor_copy(row[:, 0:1], row_i[:, :]))
                nc.vector.tensor_scalar(row[:, 1:2], row[:, 0:1], float(P), None, ALU.add)
                nc.vector.tensor_scalar(ident[:, :], col[:, 0:P], row[:, 0:1], None, ALU.is_equal)
                nc.vector.tensor_scalar(before[:, :], col[:, 0:P], row[:, 0:1], None, ALU.is_gt)
                link(nc.vector.tensor_scalar(after[:, :], col[:, 0:P], row[:, 0:1], None, ALU.is_lt))
                nc.vector.tensor_scalar(ints2[:, 0, 0:1], row_i[:, :], 1, None, ALU.bitwise_and).then_inc(cols, 1)
                dve.wait_ge(cols, 3)
                link(nc.vector.tensor_copy(odd[:, 0:1], ints2[:, 0, 0:1]))
                nc.vector.tensor_scalar(odd[:, 1:2], odd[:, 0:1], -float(OVER), None, ALU.mult)
                nc.vector.tensor_scalar(odd[:, 2:3], odd[:, 0:1], -float(OVER), float(P), ALU.mult, ALU.add)
                nc.vector.tensor_scalar(odd[:, 3:4], row[:, 0:1], float(OVER), float(P), ALU.is_ge, ALU.mult)
                link(nc.vector.tensor_copy(col_win[:, 0:P], col[:, 0:P]))
                nc.vector.tensor_scalar(fl[:, 0, 0:P], col[:, 0:P], float(OVER), odd[:, 0:1], ALU.is_ge, ALU.not_equal)
                link(nc.vector.tensor_scalar(fl2[:, 0, 0:P], col[:, P:2 * P], odd[:, 1:2], None, ALU.add))
                link(nc.vector.scalar_tensor_tensor(col_win[:, P:2 * P], fl[:, 0, 0:P], float(NOWHERE), fl2[:, 0, 0:P],
                                                    ALU.mult, ALU.add))
                dve.wait_ge(loaded, 16 * (len(CHALF) + (EL < P)))
                nc.vector.tensor_scalar(ints2[:, :, 0:P], ints[:, :, 0:P], 7, None, ALU.arith_shift_right)
                link(nc.vector.tensor_scalar(ints2[:, :, P:2 * P], ints[:, :, 0:P], P - 1, None, ALU.bitwise_and))
                nc.vector.tensor_copy(fl[:, :, :], ints2[:, :, :]).then_inc(turned, 1)
                dve.wait_ge(turned, 2)
                nc.vector.tensor_copy(hi_t[:, :], bank[0][:, 0:NC])
                link(nc.vector.tensor_copy(lo_t[:, :], bank[1][:, 0:NC]))
                def one_hot(t, known):
                    if known is None or known >= 4:
                        dve.wait_ge(hot_used, t.n - 3)
                    nc.vector.tensor_scalar(oh_lo[t.u][:, :], colb[:, 0:P], lo_t[:, bass.ds(t.n, 1)], None,
                                            ALU.is_equal).then_inc(hot_made, 1)
                    nc.vector.tensor_scalar(oh_hi[t.u][:, 0:NTE], colb[:, 0:NTE], hi_t[:, bass.ds(t.n, 1)], None,
                                            ALU.is_equal).then_inc(hot_made, 1)
                run_tiles(dve, NC, 4, one_hot)
                dve.wait_ge(counted, 1)
                nc.vector.tensor_copy(deg[:, :], bank[2][:, 0:NTE])
                nc.vector.tensor_scalar(deg1[:, :], bank[2][:, 0:NTE], 1.0, None, ALU.add).then_inc(counted, 1)
                dve.wait_ge(counted, 2)
                nc.vector.reciprocal(sq[:, :], deg1[:, :]).then_inc(roots, 1)
                dve.wait_ge(counted, 3)
                newton(dve, dinv, deg1, rstd_x, nr_made, 0)
                nc.vector.tensor_scalar(eps2[:, :], deg1[:, :], EPS, None, ALU.mult)
                nc.vector.tensor_tensor(sq[:, :], deg1[:, :], dinv[:, :], ALU.mult).then_inc(roots, 1)
                link(nc.vector.memset(cnt[:, :], 0.0))
                dve.wait_ge(turned, 3)
                for h, rows in THALF:
                    c = nc.vector.tensor_copy(cnt[0:rows, h:h + 1], bank[3][0:rows, h:h + 1])
                c.then_inc(turned, 1)
                dve.wait_ge(counted, 4)
                nc.vector.tensor_copy(start_i[:, 0, 0:len(THALF)], bank[4][:, 0:len(THALF)])
                nc.vector.tensor_scalar(start_i[:, 1, 0:len(THALF)], bank[4][:, 0:len(THALF)], odd[:, 2:3], None,
                                        ALU.add).then_inc(counted, 1)
                dve.wait_ge(windows, 64 * len(THALF))
                link(nc.vector.memset(seen[:, :], 0.0))
                for h, rows in THALF:
                    r = slice(0, rows)
                    link(nc.vector.tensor_copy(fl2[r, h, :], ints[r, h, :]))
                    link(nc.vector.tensor_scalar(ints[r, h, :], ints[r, h, :], 7, None, ALU.arith_shift_right))
                    link(nc.vector.tensor_copy(fl[r, h, :], ints[r, h, :]))
                    link(nc.vector.scalar_tensor_tensor(fl2[r, h, :], fl[r, h, :], -float(P), fl2[r, h, :],
                                                        ALU.mult, ALU.add))
                    link(nc.vector.tensor_scalar(fl[r, h, :], fl[r, h, :], row[r, h:h + 1], None, ALU.is_equal))
                    link(nc.vector.scalar_tensor_tensor(fl[r, h, :], col_win[r, :], cnt[r, h:h + 1], fl[r, h, :],
                                                        ALU.is_lt, ALU.mult))
                    link(nc.vector.reduce_sum(seen[r, h:h + 1], fl[r, h, :], mybir.AxisListType.X))
                link(nc.vector.tensor_tensor(ok[:, 0:1], seen[:, 0:1], seen[:, 1:2], ALU.add))
                nc.vector.tensor_copy(ok[:, 0:1], ok[:, 0:1]).then_inc(turned, 1)
                dve.wait_ge(turned, 6)
                link(nc.vector.tensor_scalar(ok[:, 1:2], bank[5][:, 0:1], float(E), None, ALU.is_equal))
                nc.vector.tensor_scalar(general[:, :], ok[:, 1:2], -1.0, 1.0, ALU.mult, ALU.add)
                for h, rows in THALF:
                    r = slice(0, rows)
                    link(nc.vector.tensor_scalar(fl[r, h, :], fl[r, h, :], ok[r, 1:2], None, ALU.mult))
                    link(nc.vector.scalar_tensor_tensor(fl2[r, h, :], fl2[r, h, :], 1.0, fl[r, h, :],
                                                        ALU.add, ALU.mult))
                nc.vector.tensor_copy(ok[:, 0:1], ok[:, 1:2]).then_inc(turned, 1)
                dve.wait_ge(turned, 8)
                over = X2t[0][:, 0:NTE]
                pairwise = over.rearrange("p (n j) -> p j n", j=2)
                nc.vector.tensor_scalar(edge_to[:, :], bank[6][:, 0:NTE], -1.0, None, ALU.add)
                link(nc.vector.tensor_copy(over, bank[7][:, 0:NTE]))
                link(nc.vector.tensor_tensor(over_to[:, :], pairwise[:, 0, :], pairwise[:, 1, :], ALU.add))
                link(nc.vector.tensor_scalar(X2t[1][:, 0:NPAIR], over_to[:, :], 0.0, odd[:, 3:4], ALU.is_gt, ALU.mult))
                nc.vector.scalar_tensor_tensor(over_to[:, :], over_to[:, :], -1.0, X2t[1][:, 0:NPAIR], ALU.add, ALU.add)
                for h, rows in THALF:
                    r = slice(0, rows)
                    link(nc.vector.tensor_copy(fl2[r, h, :], ints2[r, h, :]))
                    link(nc.vector.scalar_tensor_tensor(fl2[r, h, :], fl2[r, h, :], -float(NOWHERE), fl[r, h, :],
                                                        ALU.add, ALU.mult))
                nc.vector.tensor_copy(ok[:, 0:1], ok[:, 1:2]).then_inc(turned, 1)
                dve.wait_ge(turned, 10)
                nc.vector.tensor_scalar(edge_from[:, 0:2, :].rearrange("p j n -> p n j"),
                                        bank[6][:, 0:NTE].rearrange("p (n j) -> p n j", j=2),
                                        float(NOWHERE), None, ALU.add)
                link(nc.vector.tensor_copy(over, bank[7][:, 0:NTE]))
                nc.vector.scalar_tensor_tensor(edge_from[:, 2, :], pairwise[:, 0, :], float(NOWHERE), pairwise[:, 1, :],
                                               ALU.add, ALU.add)
                dve.wait_ge(roots, 3)
                for h, rows in THALF:
                    r = slice(0, rows)
                    nc.vector.tensor_copy(sq_hi[r, h, 0, :], bank[h][r, 0:P])
                    link(nc.vector.tensor_copy(sq_hi[r, h, 1, :], bank[h][r, 0:P]))
                    c = nc.vector.tensor_tensor(sq_hi[r, h, 2, :], bank[h][r, 0:P], sq_hi[r, h, 0, :].bitcast(F32),
                                                ALU.subtract)
                c.then_inc(roots, 1)
                dve.wait_ge(vectors, 16 * 7)
                link(nc.vector.tensor_scalar(row[:, 1:2], row[:, 0:1], 1.0, None, ALU.is_equal))
                link(nc.vector.tensor_scalar(row[:, 2:3], row[:, 1:2], -1.0, 1.0, ALU.mult, ALU.add))
                for q in range(2):
                    b = bias_b[q][0:3, :]
                    link(nc.vector.tensor_copy(b_hi[:, :], b))
                    link(nc.vector.tensor_tensor(b_lo[:, :], b, b_hi[:, :].bitcast(F32), ALU.subtract))
                    link(nc.vector.tensor_scalar(b_lo[:, :], b_lo[:, :], row[0:3, 1:2], None, ALU.mult))
                    link(nc.vector.scalar_tensor_tensor(B3[q][:, :], b_hi[:, :].bitcast(F32), row[0:3, 2:3], b_lo[:, :],
                                                        ALU.mult, ALU.add))
                for q in range(3):
                    for k in range(KD):
                        dve.wait_ge(w_split, KD * q + k + 1)
                        nc.vector.tensor_tensor(Wlo[q][:, k, :], stage[k][:, :], Whi[q][:, k, :].bitcast(F32),
                                                ALU.subtract).then_inc(w_free, 1)

            @block.tensor
            def _(pe):
                pe.wait_ge(turned, 1)
                pe.wait_ge(dve1, 5)
                for h, rows in CHALF:
                    nc.tensor.transpose(bank[0][:, h * P:h * P + rows], fl[0:rows, h, 0:P], ident[0:rows, 0:rows])
                    m = nc.tensor.transpose(bank[1][:, h * P:h * P + rows], fl[0:rows, h, P:2 * P],
                                            ident[0:rows, 0:rows])
                m.then_inc(turned, 1)

                def count(t, known):
                    pe.wait_ge(hot_made, 2 * t.n + 2)
                    m = nc.tensor.matmul(bank[2][:, 0:NTE], oh_lo[t.u][:, :], oh_hi[t.u][:, 0:NTE],
                                         start=(known == 0), stop=(known == NC - 1), skip_group_check=True)
                    m.then_inc(hot_used, 1)
                    if known == NC - 1:
                        pe.wait_ge(hot_used, NC)
                        nc.tensor.transpose(bank[7][0:P, 0:P], ident[:, :], ident[:, :]).then_inc(counted, 1)
                run_tiles(pe, NC, 4, count)
                pe.wait_ge(counted, 2)
                for h, rows in THALF:
                    m = nc.tensor.matmul(bank[3][0:rows, h:h + 1], deg[:, h * P:h * P + rows], ones[:, 0:1],
                                         start=True, stop=True, skip_group_check=True)
                m.then_inc(turned, 1)
                pe.wait_ge(turned, 4)
                for h, _ in THALF:
                    m = nc.tensor.matmul(bank[4][:, h:h + 1], before[:, :], cnt[:, h:h + 1], start=True, stop=(h == 0),
                                         skip_group_check=True)
                    if h:
                        m = nc.tensor.matmul(bank[4][:, h:h + 1], ones[:, :], cnt[:, 0:1], start=False, stop=True,
                                             skip_group_check=True)
                m.then_inc(counted, 1)
                pe.wait_ge(turned, 5)
                nc.tensor.matmul(bank[5][:, 0:1], ones[:, :], ok[:, 0:1], start=True, stop=True).then_inc(turned, 1)
                pe.wait_ge(roots, 2)
                for h, rows in THALF:
                    m = nc.tensor.transpose(bank[h][0:rows, 0:P], sq[:, h * P:h * P + rows], ident[:, :])
                m.then_inc(roots, 1)
                for filled in (7, 9):
                    pe.wait_ge(turned, filled)
                    for k in range(2):
                        for h, rows in THALF:
                            m = nc.tensor.transpose(bank[6 + k][:, h * P:h * P + rows],
                                                    fl2[0:rows, h, k * P:(k + 1) * P], ident[0:rows, 0:rows])
                    m.then_inc(turned, 1)

        X_SLOTS = 4
        NX = [*SelfP, *XtP]
        x_in = [sem(f"x_in{u}") for u in range(X_SLOTS)]
        st_made, ag_made, co_made = sem("n_stats"), sem("n_mean_var"), sem("n_coefs")
        mv_kept, co_turned, co_out = sem("n_kept"), sem("n_coefs_turned"), sem("n_coefs_out")
        turned_co = YP[0][:, :, 0:2 * P].rearrange("p h (j k) -> p h j k", k=2)

        with nc.Block() as block:
            @block.sync
            def _(sp):
                def load(p, known):
                    if known is None or known >= X_SLOTS:
                        sp.wait_ge(st_made, (p.n - X_SLOTS) * 2 + 2)
                    if known == NPAIR - 1:
                        sp.dma_start(NX[p.u][0:LAST, 0, :], x[(NT - 1) * P:N, :]).then_inc(x_in[p.u], 16)
                    else:
                        sp.dma_start(NX[p.u][:, :, :], x[bass.ds(p.n * 2 * P, 2 * P), :]
                                     .rearrange("(j p) d -> p j d", p=P)).then_inc(x_in[p.u], 16)
                run_tiles(sp, NPAIR, X_SLOTS, load)
                for u in range(X_SLOTS):
                    sp.wait_ge(x_in[u], 16 * len(range(u, NPAIR, X_SLOTS)))
                sp.wait_ge(co_made, 5 + 2 * len(THALF))
                for h, rows in THALF:
                    sp.dma_start(COEF[h * P * P:(h * P + rows) * P, :].rearrange("(t j) k -> t j k", j=P),
                                 turned_co[0:rows, h, :, :]).then_inc(co_out, 16)
                sp.wait_ge(co_out, 16 * len(THALF))

            @block.vector
            def _(dve):
                def mean_var(p, n_tiles=2):
                    m = small[p.u]
                    dve.wait_ge(st_made, p.n * 2 + n_tiles)
                    dve.sem_inc(aggr_go, 1)
                    for j in range(n_tiles):
                        a = nc.vector.bn_aggr(m[:, 12 + 2 * j:14 + 2 * j], m[:, 6 * j:6 * j + 6])
                    a.then_inc(ag_made, 1)

                def keep(p, n_tiles=2):
                    dve.wait_ge(ag_made, p.n + 1)
                    nc.vector.tensor_copy(mv_x[:, bass.ds(p.n * 2, n_tiles), :],
                                          small[p.u][:, 12:12 + 2 * n_tiles].rearrange("p (j k) -> p j k", k=2))\
                        .then_inc(mv_kept, 1)

                def stats(p, known):
                    n_tiles = 1 if known == NPAIR - 1 else 2
                    m = small[p.u]
                    dve.wait_ge(x_in[p.u], 16 * (p.i + 1))
                    if known is None or known >= X_SLOTS:
                        dve.wait_ge(mv_kept, p.n - X_SLOTS + 1)
                    for j in range(n_tiles):
                        nc.vector.bn_stats(m[:, 6 * j:6 * j + 6], NX[p.u][:, j, :]).then_inc(st_made, 1)
                    if known not in (0, 1):
                        keep(p.after(-2))
                    if known != 0:
                        mean_var(p.after(-1))
                    if known == NPAIR - 1:
                        keep(p.after(-1))
                        mean_var(p, 1)
                        keep(p, 1)
                run_tiles(dve, NPAIR, X_SLOTS, stats)
                dve.wait_ge(mv_kept, NPAIR)
                nc.vector.tensor_scalar(off_h[:, :], mv_x[:, :, 1], EPS, None, ALU.add).then_inc(co_made, 1)
                dve.wait_ge(co_made, 1)
                nc.vector.reciprocal(nb_x[:, :], off_h[:, :]).then_inc(co_made, 1)
                dve.wait_ge(co_made, 3)
                newton(dve, rstd_x, off_h, scale_h, nr_made, 4)
                nc.vector.scalar_tensor_tensor(nb_x[:, :], mv_x[:, :, 0], -1.0, rstd_x[:, :], ALU.mult, ALU.mult)
                nc.vector.tensor_tensor(scale_h[:, :], rstd_x[:, :], dinv[:, :], ALU.mult).then_inc(co_made, 1)
                dve.wait_ge(co_made, 4)
                nc.vector.scalar_tensor_tensor(off_h[:, :], mv_x[:, :, 0], -1.0, scale_h[:, :], ALU.mult, ALU.mult)\
                    .then_inc(co_made, 1)
                dve.wait_ge(co_turned, 2)
                for k in range(2):
                    for h, rows in THALF:
                        nc.vector.tensor_copy(turned_co[0:rows, h, :, k], bank[2 * h + k][0:rows, 0:P])\
                            .then_inc(co_made, 1)

            @block.scalar
            def _(act):
                act.wait_ge(co_made, 2)
                nc.scalar.activation(rstd_x[:, :], nb_x[:, :], ACT.Sqrt).then_inc(co_made, 1)

            @block.tensor
            def _(pe):
                for k, table in enumerate((scale_h, off_h)):
                    pe.wait_ge(co_made, 4 + k)
                    for h, rows in THALF:
                        m = nc.tensor.transpose(bank[2 * h + k][0:rows, 0:P], table[:, h * P:h * P + rows], ident[:, :])
                    m.then_inc(co_turned, 1)

        def if_general(engine, program):
            flag = engine.value_load(general[0:1, 0:1], min_val=0, max_val=1)
            with engine.If(flag > 0):
                program(engine)
            return flag

        gx_in, gh_made, gh_out = sem("g_x_in"), sem("g_h_made"), sem("g_h_out")
        with nc.Block() as block:
            @block.sync
            def _(sp):
                def step(t, rows, start=False):
                    if not start:
                        sp.wait_ge(gh_out, 16 * t)
                    sp.dma_start(Xt[0][0:rows, :], x[bass.ds(t * P, rows), :]).then_inc(gx_in, 16)
                    sp.wait_ge(gh_made, t + 1)
                    sp.dma_start(H[0][bass.ds(t * P, rows), :], Ho[0][0:rows, :]).then_inc(gh_out, 16)

                def program(sp):
                    step(0, P, start=True)
                    with sp.Fori(1, NT - 1) as t:
                        step(t, P)
                    step(NT - 1, LAST)
                    sp.wait_ge(gh_out, 16 * NT)
                if_general(sp, program)

            @block.scalar
            def _(act):
                def program(act):
                    with act.Fori(0, NT) as t:
                        act.wait_ge(gx_in, 16 * (t + 1))
                        nc.scalar.activation(Ho[0], Xt[0], ACT.Relu, bias=off_h[:, bass.ds(t, 1)],
                                             scale=scale_h[:, bass.ds(t, 1)]).then_inc(gh_made, 1)
                if_general(act, program)

            @block.vector
            def _(dve):
                def program(dve):
                    dve.wait_ge(gh_made, NT)
                    nc.vector.memset(scale_h[:, :], 1.0)
                    nc.vector.memset(off_h[:, :], 0.0)
                if_general(dve, program)

        gather_go = sem("gather_go")
        g_copied, g_idx, g_rows, g_add = sem("g_copied"), sem("g_indices"), sem("g_rows"), sem("g_added")
        g_step, g_sum, g_to = sem("g_step"), sem("g_summed"), sem("g_targets")

        def general_sums(q):
            def k(c):
                return q * NC + c

            row_dst, M, Gs, Sum = Cv[0][:, 0:P], Cv[1], Y[0], Y[1]
            row_i32 = ints[:, 0, 0:P]
            def general_sync(sp):
                sp.dma_start(H[q][ROWS:ROWS + (NT - 1) * P, :], H[q][0:(NT - 1) * P, :]).then_inc(g_copied, 16)
                sp.dma_start(H[q][ROWS + (NT - 1) * P:ROWS + N, :], H[q][(NT - 1) * P:N, :]).then_inc(g_copied, 16)
                for z in range(2):
                    sp.dma_start(H[q][ROWS + NP + z * P:ROWS + NP + (z + 1) * P, :], G[0][:, 0, :])\
                        .then_inc(g_copied, 16)
                sp.wait_ge(g_copied, 64 * (q + 1))

                def fetch(c):
                    sp.dma_start(ints2[:, 0, 0:1], SRC[bass.ds(c * P, P), :]).then_inc(g_idx, 16)
                    sp.dma_start(ints2[:, 0, 1:2], DST[bass.ds(c * P, P), :]).then_inc(g_idx, 16)
                    sp.dma_start(row_i32, DST[bass.ds(c * P, P), :].rearrange("j o -> o j").broadcast_to([P, P]))\
                        .then_inc(g_idx, 16)

                fetch(0)
                with sp.Fori(1, NC) as c:
                    sp.wait_ge(g_add, 16 * k(c))
                    fetch(c)
                sp.wait_ge(g_add, 16 * k(NC))

            def general_pool(pool):
                last_row, last_sum = pool.to_reg(N - 1), pool.to_reg(2 * ROWS - 1)
                pool.wait_ge(g_copied, 64 * (q + 1))
                with pool.Fori(0, NC) as c:
                    pool.wait_ge(g_idx, 48 * (k(c) + 1))
                    pool.sem_inc(gather_go, 1)
                    pool.indirect_dma_start(Gs[:, :], None, H[q][0:N, :],
                                            bass.IndirectOffsetOnAxis(ap=ints2[:, 0, 0:1], axis=0),
                                            bounds_check=last_row, oob_is_err=False).then_inc(g_rows, 16)
                    pool.wait_ge(g_to, k(c) + 1)
                    pool.sem_inc(gather_go, 1)
                    pool.indirect_dma_start(H[q], bass.IndirectOffsetOnAxis(ap=ints2[:, 1, 0:1], axis=0),
                                            Sum[:, :], None, bounds_check=last_sum,
                                            compute_op=ALU.add).then_inc(g_add, 16)
                pool.wait_ge(g_add, 16 * k(NC))

            def general_vector(dve):
                with dve.Fori(0, NC) as c:
                    s = 7 * k(c)
                    dve.wait_ge(g_idx, 48 * (k(c) + 1))
                    nc.vector.tensor_copy(row_dst, row_i32)
                    nc.vector.tensor_copy(M[:, 2 * P:2 * P + 1], ints2[:, 0, 1:2]).then_inc(g_step, 1)
                    dve.wait_ge(g_step, s + 1)
                    nc.vector.tensor_scalar(M[:, 0:P], row_dst, M[:, 2 * P:2 * P + 1], None, ALU.is_equal)\
                        .then_inc(g_step, 1)
                    dve.wait_ge(g_step, s + 2)
                    nc.vector.tensor_tensor(M[:, P:2 * P], M[:, 0:P], after[:, :], ALU.mult).then_inc(g_step, 1)
                    dve.wait_ge(g_step, s + 3)
                    nc.vector.reduce_sum(M[:, 2 * P + 1:2 * P + 2], M[:, P:2 * P], mybir.AxisListType.X)\
                        .then_inc(g_step, 1)
                    dve.wait_ge(g_step, s + 4)
                    nc.vector.tensor_scalar(M[:, 2 * P + 2:2 * P + 3], M[:, 2 * P + 1:2 * P + 2], 0.0, None,
                                            ALU.is_equal)
                    nc.vector.tensor_scalar(M[:, 2 * P + 3:2 * P + 4], row[:, 0:1], -1.0, -float(TRASH),
                                            ALU.mult, ALU.add).then_inc(g_step, 1)
                    dve.wait_ge(g_step, s + 5)
                    nc.vector.tensor_tensor(M[:, 2 * P + 4:2 * P + 5], M[:, 2 * P:2 * P + 1],
                                            M[:, 2 * P + 3:2 * P + 4], ALU.add).then_inc(g_step, 1)
                    dve.wait_ge(g_step, s + 6)
                    nc.vector.scalar_tensor_tensor(M[:, 2 * P + 5:2 * P + 6], M[:, 2 * P + 4:2 * P + 5],
                                                   M[:, 2 * P + 2:2 * P + 3], M[:, 2 * P + 3:2 * P + 4],
                                                   ALU.mult, ALU.subtract).then_inc(g_step, 1)
                    dve.wait_ge(g_step, s + 7)
                    nc.vector.tensor_scalar(ints2[:, 1, 0:1], M[:, 2 * P + 5:2 * P + 6], float(ROWS), None,
                                            ALU.add)
                    dve.wait_ge(g_sum, k(c) + 1)
                    nc.vector.tensor_copy(Sum[:, :], bank[6][:, :]).then_inc(g_to, 1)
                dve.wait_ge(g_add, 16 * k(NC))

            def general_tensor(pe):
                with pe.Fori(0, NC) as c:
                    pe.wait_ge(g_rows, 16 * (k(c) + 1))
                    pe.wait_ge(g_step, 7 * k(c) + 2)
                    nc.tensor.matmul(bank[6][:, :], M[:, 0:P], Gs[:, :], start=True, stop=True)\
                        .then_inc(g_sum, 1)

            return general_sync, general_pool, general_vector, general_tensor

        def slot_sems(name):
            return [sem(f"{name}{u}") for u in range(PAIRS)]

        self_in, edge_in, xt_in = slot_sems("self_in"), slot_sems("edge_in"), slot_sems("xt_in")
        coef_in = slot_sems("coef_in")
        root_in, ho_out, xo_out = slot_sems("root_in"), slot_sems("ho_out"), slot_sems("xo_out")
        nodes_made, edges_made, over_made = sem("nodes_made"), sem("edges_made"), sem("over_made")
        idx_made, s_made, agg_done = sem("idx_made"), sem("s_made"), sem("agg_done")
        hi_done, lo_done, vhi_done, vlo_done = sem("hi_done"), sem("lo_done"), sem("vhi_done"), sem("vlo_done")
        main_done, stats_done, mv_done, ve_done = sem("main_done"), sem("stats_done"), sem("mv_done"), sem("ve_done")
        rstd_done, cg_done, y_done, gelu_done = sem("rstd_done"), sem("cg_done"), sem("y_done"), sem("gelu_done")
        h_done, r_done, rb_done = sem("h_done"), sem("r_done"), sem("rb_done")
        x2_done, mean2_done, sq2_done, sc2_done = sem("x2_done"), sem("mean2_done"), sem("sq2_done"), sem("sc2_done")
        co2_done, xb_done, res_done = sem("co2_done"), sem("xb_done"), sem("res_done")

        def convolution(q):
            first, second, third = q == 0, q == 1, q == 2

            def total(t):
                return NT if t.slots == SLOTS else NPAIR

            def uses(t, a_phase=q):
                return a_phase * len(range(t.u, total(t), t.slots)) + t.i + 1

            def upto(t, phase=q):
                return phase * total(t) + t.n + 1

            def wait_free(engine, s, t, known, phase=q):
                if known is not None and known < t.slots:
                    if phase:
                        engine.wait_ge(s, phase * total(t))
                else:
                    engine.wait_ge(s, phase * total(t) + t.n - t.slots + 1)

            def shifted(known, k):
                return None if known is None else known + k

            def tile(p, j):
                return Tile(p.i, 2 * p.u + j, SLOTS)

            def tiles(p, known):
                for j in range(2):
                    n = None if known is None else 2 * known + j
                    if n is None or n < NT:
                        yield tile(p, j), n

            general_sync, general_pool, general_vector, general_tensor = general_sums(q)

            with nc.Block() as block:
                @block.sync
                def _(sp):
                    general_reg = if_general(sp, general_sync)

                    def move(p, known, buffer, rows, base, inward):
                        if known == NPAIR - 1:
                            sbuf, dram = buffer[0:LAST, 0, :], rows[bass.ds(base + p.n * 2 * P, LAST), :]
                        else:
                            sbuf = buffer[:, :, :]
                            dram = rows[bass.ds(base + p.n * 2 * P, 2 * P), :].rearrange("(j p) d -> p j d", p=P)
                        return sp.dma_start(sbuf, dram) if inward else sp.dma_start(dram, sbuf)

                    def last_tile(p, known):
                        return tile(p, 0 if known == NPAIR - 1 else 1)

                    def load_self(p, known, use_x):
                        wait_free(sp, nodes_made if first else agg_done, p, known)
                        if use_x:
                            move(p, known, SelfP[p.u], x, 0, True).then_inc(self_in[p.u], 16)
                        else:
                            base = ROWS if first else general_reg * ROWS
                            move(p, known, SelfP[p.u], H[q], base, True).then_inc(self_in[p.u], 16)

                    def pair_free(s, p, known, phase):
                        if known is not None and known < PAIRS:
                            if phase:
                                sp.wait_ge(s, phase * NT)
                        else:
                            sp.wait_ge(s, phase * NT + 2 * (p.n - PAIRS) + 2)

                    def load_root(p, known):
                        if not third:
                            pair_free(main_done, p, known, q)
                            sp.dma_start(root[p.u][:, :, :].bitcast(F32), SQ[bass.ds(p.n * 2, 2), :]
                                         .rearrange("o (a j) -> a o j", a=3)).then_inc(root_in[p.u], 16)

                    def load_x(p, known):
                        if second:
                            pair_free(x2_done, p, known, 0)
                            move(p, known, XtP[p.u], x, 0, True).then_inc(xt_in[p.u], 16)
                        if third:
                            pair_free(xb_done, p, known, 0)
                            move(p, known, XtP[p.u], X2, 0, True).then_inc(xt_in[p.u], 16)

                    def store_x(p, known):
                        t = last_tile(p, known)
                        if second:
                            sp.wait_ge(x2_done, upto(t, 0))
                            move(p, known, X2P[p.u], X2, 0, False).then_inc(xo_out[p.u], 16)
                        if third:
                            sp.wait_ge(res_done, upto(t, 0))
                            move(p, known, CvP[p.u], out, 0, False).then_inc(xo_out[p.u], 16)

                    def store_h(p, known):
                        if not third:
                            sp.wait_ge(h_done, upto(last_tile(p, known)))
                            move(p, known, HoP[p.u], H[q + 1], 0, False).then_inc(ho_out[p.u], 16)

                    def body(p, known, use_x=False):
                        if known == 0:
                            load_self(p, 0, use_x)
                            load_root(p, 0)
                            load_x(p, 0)
                            for k in (1, 2):
                                load_self(p.after(k), k, use_x)
                        if known != NPAIR - 1:
                            load_root(p.after(1), shifted(known, 1))
                        if known is None or known + 3 < NPAIR:
                            load_self(p.after(3), shifted(known, 3), use_x)
                        if known != NPAIR - 1:
                            load_x(p.after(1), shifted(known, 1))
                        if known != 0:
                            store_x(p.after(-1), shifted(known, -1))
                        if known != 0:
                            store_h(p.after(-1), shifted(known, -1))
                        if known == NPAIR - 1:
                            store_x(p, known)
                            store_h(p, known)
                    if first:
                        with sp.If(general_reg > 0):
                            run_tiles(sp, NPAIR, PAIRS, body, 3)
                        with sp.If(general_reg < 1):
                            run_tiles(sp, NPAIR, PAIRS, lambda p, known: body(p, known, True), 3)
                    else:
                        run_tiles(sp, NPAIR, PAIRS, body, 3)
                    for u in range(PAIRS):
                        n = len(range(u, NPAIR, PAIRS))
                        if not third:
                            sp.wait_ge(ho_out[u], 16 * (q + 1) * n)
                        if not first:
                            sp.wait_ge(xo_out[u], 16 * q * n)

                @block.gpsimd
                def _(pool):
                    if_general(pool, general_pool)

                    def gather(p, known):
                        if known is None or known >= PAIRS:
                            pool.wait_ge(edge_in[p.u], 16 * CHUNKS * (uses(p) - 1))
                            if first:
                                pool.wait_ge(coef_in[p.u], 16 * CHUNKS * (uses(p) - 1))
                        nc.gpsimd.tensor_copy(idx[p.u][:, :], edge_from[:, :, bass.ds(p.n, 1)]
                                              .rearrange("p k o -> p (k o)")).then_inc(idx_made, 1)
                        wait_free(pool, edges_made if first else agg_done, p, known)
                        pool.wait_ge(idx_made, upto(p))
                        pool.sem_inc(gather_go, 1)
                        for k in range(CHUNKS):
                            pool.indirect_dma_start(G[p.u][:, k, :], None, x if first else H[q][0:N, :],
                                                    bass.IndirectOffsetOnAxis(ap=idx[p.u][:, k:k + 1], axis=0),
                                                    bounds_check=N - 1, oob_is_err=False).then_inc(edge_in[p.u], 16)

                    def gather_coefs(p):
                        for k in range(CHUNKS):
                            pool.indirect_dma_start(edge_co[p.u][:, k, :], None, COEF[0:N, :],
                                                    bass.IndirectOffsetOnAxis(ap=idx[p.u][:, k:k + 1], axis=0),
                                                    bounds_check=N - 1, oob_is_err=False).then_inc(coef_in[p.u], 16)

                    def residual(t, known):
                        if second:
                            pool.wait_ge(r_done, upto(t, 0))
                            nc.gpsimd.tensor_tensor(R[t.u], R[t.u], beta_b[1][:, :], ALU.add)\
                                .then_inc(rb_done, 1)
                        if third:
                            pool.wait_ge(xt_in[t.u // 2], 16 * (uses(Tile(t.i, t.u // 2, PAIRS), 1)))
                            wait_free(pool, res_done, t, known, 0)
                            nc.gpsimd.tensor_tensor(R[t.u], Xt[t.u], bias_b[2][:, :], ALU.add)\
                                .then_inc(xb_done, 1)

                    def power(t, known):
                        m = small[t.u]
                        late = second and known not in (0, 1)
                        c = slice(8, 25, 16) if late else slice(8, 9)
                        d = slice(9, 26, 16) if late else slice(9, 10)
                        pool.wait_ge(ve_done, upto(t))
                        nc.gpsimd.tensor_tensor(m[:, d], m[:, c], neg_half[:, 0:1 + late], ALU.pow)\
                            .then_inc(rstd_done, 1)

                    def body(p, known):
                        if known == 0:
                            for k in range(3):
                                gather(p.after(k), k)
                                if first:
                                    gather_coefs(p.after(k))
                        if known is None or known + 3 < NPAIR:
                            gather(p.after(3), shifted(known, 3))
                        for t, n in tiles(p, known):
                            if not first:
                                residual(t, n)
                            if not third:
                                power(t, n)
                            if first and t.u % 2 == 0 and (known is None or known + 3 < NPAIR):
                                gather_coefs(p.after(3))
                            if second and n == NT - 1:
                                for k in (1, 2):
                                    m = small[t.after(k).u]
                                    pool.wait_ge(ve_done, upto(t) + k)
                                    nc.gpsimd.tensor_tensor(m[:, 25:26], m[:, 24:25], neg_half[:, 0:1], ALU.pow)\
                                        .then_inc(rstd_done, 1)
                    run_tiles(pool, NPAIR, PAIRS, body, 3)

                @block.scalar
                def _(act):
                    def make_nodes(p, known):
                        wait_free(act, agg_done, p, known)
                        act.wait_ge(self_in[p.u], 16 * uses(p))
                        for j in range(2):
                            c = bass.ds(tile(p, j).n, 1)
                            m = nc.scalar.activation(XH[p.u][:, j, :], SelfP[p.u][:, j, :], ACT.Relu, bias=off_h[:, c],
                                                     scale=scale_h[:, c])
                        m.then_inc(nodes_made, 1)

                    def make_edge_rows(p, k, o):
                        return nc.scalar.activation(o, G[p.u][:, k, :], ACT.Relu, bias=edge_co[p.u][:, k, 1:2],
                                                    scale=edge_co[p.u][:, k, 0:1])

                    def over_high(p, known):
                        act.wait_ge(edge_in[p.u], 16 * CHUNKS * uses(p))
                        wait_free(act, agg_done, p, known)
                        if first:
                            act.wait_ge(coef_in[p.u], 16 * CHUNKS * uses(p))
                            make_edge_rows(p, 2, VH[p.u]).then_inc(over_made, 1)
                            act.wait_ge(over_made, upto(p))
                        nc.scalar.activation(Vhi[p.u][:, :], VH[p.u] if first else G[p.u][:, 2, :], ACT.Copy)\
                            .then_inc(vhi_done, 1)
                        if first:
                            make_edge_rows(p, 0, RH[p.u][:, 0, :])
                            make_edge_rows(p, 1, RH[p.u][:, 1, :]).then_inc(edges_made, 1)

                    def high(p):
                        act.wait_ge(agg_done, upto(p))
                        nc.scalar.activation(Ahi[p.u][:, :], Agg[p.u][:, :], ACT.Copy).then_inc(hi_done, 1)

                    def relu_x(t, known):
                        act.wait_ge(xt_in[t.u // 2], 16 * uses(Tile(t.i, t.u // 2, PAIRS), 0))
                        wait_free(act, y_done, t, known)
                        nc.scalar.activation(R[t.u], Xt[t.u], ACT.Relu, bias=nb_x[:, bass.ds(t.n, 1)],
                                             scale=rstd_x[:, bass.ds(t.n, 1)]).then_inc(r_done, 1)

                    def wait_stored(t, known):
                        if known is None or known >= SLOTS:
                            act.wait_ge(ho_out[t.u // 2], 16 * (uses(Tile(t.i, t.u // 2, PAIRS)) - 1))

                    def squares(t):
                        m = small[t.after(2).u]
                        act.wait_ge(mean2_done, upto(t, 0))
                        nc.scalar.activation(Y[t.u], X2t[t.u], ACT.Square, bias=m[:, 22:23],
                                             accum_out=m[:, 17:18]).then_inc(sq2_done, 1)

                    def scale(t, known):
                        wait_stored(t, known)
                        act.wait_ge(gelu_done, upto(t))
                        nc.scalar.activation(Ho[t.u], Y[t.u], ACT.Copy,
                                             scale=dinv[:, bass.ds(t.n, 1)]).then_inc(h_done, 1)

                    def relu_x2(t, known):
                        m = small[t.after(2).u]
                        act.wait_ge(co2_done, upto(t, 0))
                        wait_stored(t, known)
                        nc.scalar.activation(Ho[t.u], X2t[t.u], ACT.Relu, bias=m[:, 27:28],
                                             scale=m[:, 26:27]).then_inc(h_done, 1)

                    def body(p, known):
                        if known == 0:
                            if first:
                                make_nodes(p, 0)
                                make_nodes(p.after(1), 1)
                            over_high(p, 0)
                            over_high(p.after(1), 1)
                            high(p)
                            if first:
                                make_nodes(p.after(2), 2)
                            else:
                                over_high(p.after(2), 2)
                            if second:
                                relu_x(tile(p, 0), 0)
                        if known != NPAIR - 1:
                            high(p.after(1))
                        if first and (known is None or known + 2 < NPAIR):
                            over_high(p.after(2), shifted(known, 2))
                        if first and known != 0:
                            scale(tile(p.after(-1), 1), None if known is None else 2 * known - 1)
                        for t, n in tiles(p, known):
                            if not first and t.u % 2 and (known is None or known + 3 < NPAIR):
                                over_high(p.after(3), shifted(known, 3))
                            if second and n != 0:
                                squares(t.after(-1))
                            if not third:
                                act.wait_ge(y_done, upto(t))
                                nc.scalar.activation(Y[t.u], Y[t.u], ACT.Gelu).then_inc(gelu_done, 1)
                            if second and n != NT - 1:
                                relu_x(t.after(1), shifted(n, 1))
                            if second and n not in (0, 1):
                                relu_x2(t.after(-2), shifted(n, -2))
                            if first:
                                if t.u % 2 == 0:
                                    scale(t, n)
                                if t.u % 2 == 0 and (known is None or known + 3 < NPAIR):
                                    make_nodes(p.after(3), shifted(known, 3))
                            if second and n == NT - 1:
                                squares(t)
                                relu_x2(t.after(-1), n - 1)
                                relu_x2(t, n)
                    run_tiles(act, NPAIR, PAIRS, body, 3)

                @block.vector
                def _(dve):
                    if_general(dve, general_vector)

                    def select(p, known):
                        wait_free(dve, agg_done, p, known)
                        for j in range(2):
                            nc.vector.tensor_scalar(S[p.u][:, j, :], col[:, 0:P], edge_to[:, bass.ds(tile(p, j).n, 1)],
                                                    None, ALU.is_equal)
                        nc.vector.tensor_scalar(Sv[p.u][:, :], col[:, :], over_to[:, bass.ds(p.n, 1)],
                                                None, ALU.is_equal).then_inc(s_made, 1)

                    def over_low(p):
                        dve.wait_ge(vhi_done, upto(p))
                        rows = VH[p.u] if first else G[p.u][:, 2, :]
                        nc.vector.tensor_tensor(Vlo[p.u][:, :], rows, Vhi[p.u][:, :].bitcast(F32),
                                                ALU.subtract).then_inc(vlo_done, 1)

                    def low(p):
                        dve.wait_ge(hi_done, upto(p))
                        nc.vector.tensor_tensor(Alo[p.u][:, :], Agg[p.u][:, :], Ahi[p.u][:, :].bitcast(F32),
                                                ALU.subtract).then_inc(lo_done, 1)

                    def x2_sum(t, known):
                        dve.wait_ge(gelu_done, upto(t))
                        if known is None or known >= SLOTS:
                            dve.wait_ge(xo_out[t.u // 2], 16 * (uses(Tile(t.i, t.u // 2, PAIRS), 0) - 1))
                            dve.wait_ge(h_done, upto(t) - SLOTS)
                            dve.wait_ge(sq2_done, upto(t, 0) - SLOTS)
                        m = small[t.after(2).u]
                        nc.vector.scalar_tensor_tensor(X2t[t.u], Xt[t.u], 1.0, Y[t.u], ALU.mult, ALU.add,
                                                       accum_out=m[:, 16:17]).then_inc(x2_done, 1)

                    def x2_mean(t):
                        m = small[t.after(2).u]
                        dve.wait_ge(x2_done, upto(t, 0))
                        nc.vector.tensor_scalar(m[:, 22:23], m[:, 16:17], -1.0 / D, None, ALU.mult)\
                            .then_inc(mean2_done, 1)

                    def x2_var_eps(t):
                        m = small[t.after(2).u]
                        dve.wait_ge(sq2_done, upto(t, 0))
                        return nc.vector.tensor_scalar(m[:, 24:25], m[:, 17:18], 1.0 / D, EPS, ALU.mult, ALU.add)

                    def x2_scale(t):
                        m = small[t.after(2).u]
                        nc.vector.tensor_tensor(m[:, 26:27], m[:, 25:26], dinv[:, bass.ds(t.n, 1)], ALU.mult)\
                            .then_inc(sc2_done, 1)

                    def x2_offset(t):
                        m = small[t.after(2).u]
                        dve.wait_ge(sc2_done, upto(t, 0))
                        nc.vector.tensor_tensor(m[:, 27:28], m[:, 22:23], m[:, 26:27], ALU.mult)\
                            .then_inc(co2_done, 1)

                    def var_eps(t):
                        m = small[t.u]
                        dve.wait_ge(mv_done, upto(t))
                        nc.vector.tensor_tensor(m[:, 8:9], m[:, 7:8], eps2[:, bass.ds(t.n, 1)], ALU.add)\
                            .then_inc(ve_done, 1)

                    def chain(t, known, fill_early, fill):
                        m = small[t.u]
                        late = second and known not in (0, 1)
                        prev = t.after(-1)
                        dve.wait_ge(main_done, upto(t))
                        if third:
                            dve.wait_ge(xb_done, upto(t, 0))
                            if known is None or known >= SLOTS:
                                dve.wait_ge(xo_out[t.u // 2], 16 * (uses(Tile(t.i, t.u // 2, PAIRS), 1) - 1))
                            nc.vector.scalar_tensor_tensor(Cv[t.u], Out[t.u][:, :], dinv[:, bass.ds(t.n, 1)],
                                                           R[t.u], ALU.mult, ALU.add).then_inc(res_done, 1)
                            fill_early()
                            fill()
                            return
                        nc.vector.bn_stats(m[:, 0:6], Out[t.u][:, :]).then_inc(stats_done, 1)
                        if second:
                            fill_early()
                            if known != 0:
                                x2_sum(prev, shifted(known, -1))
                        dve.wait_ge(stats_done, upto(t))
                        dve.sem_inc(aggr_go, 1)
                        nc.vector.bn_aggr(m[:, 6:8], m[:, 0:6]).then_inc(mv_done, 1)
                        if late:
                            x2_var_eps(t.after(-2))
                        var_eps(t)
                        if second and known != 0:
                            x2_mean(prev)
                        nc.vector.scalar_tensor_tensor(Cv[t.u], Out[t.u][:, :], m[:, 6:7], gamma_b[q][:, :],
                                                       ALU.subtract, ALU.mult).then_inc(cg_done, 1)
                        if not second:
                            fill_early()
                        fill()
                        dve.wait_ge(rstd_done, upto(t))
                        if late:
                            x2_scale(t.after(-2))
                        dve.wait_ge(cg_done, upto(t))
                        if first:
                            wait_free(dve, h_done, t, known)
                            plus = beta_b[0][:, :]
                        else:
                            dve.wait_ge(rb_done, upto(t, 0))
                            plus = R[t.u]
                        nc.vector.scalar_tensor_tensor(Y[t.u], Cv[t.u], m[:, 9:10], plus,
                                                       ALU.mult, ALU.add).then_inc(y_done, 1)
                        if late:
                            x2_offset(t.after(-2))
                        if second and known == NT - 1:
                            x2_sum(t, known)
                            x2_mean(t)
                            for k in (1, 2):
                                x2_var_eps(t.after(k - 2)).then_inc(ve_done, 1)
                                dve.wait_ge(rstd_done, upto(t) + k)
                                x2_scale(t.after(k - 2))
                                x2_offset(t.after(k - 2))

                    def body(p, known):
                        if known == 0:
                            for k in range(3):
                                select(p.after(k), k)
                                if k == 0:
                                    over_low(p)
                                    low(p)
                                elif k == 1 or not first:
                                    over_low(p.after(k))

                        def nothing():
                            pass

                        def low_next():
                            if known != NPAIR - 1:
                                low(p.after(1))

                        def select_ahead():
                            if known is None or known + 3 < NPAIR:
                                select(p.after(3), shifted(known, 3))

                        def over_low_ahead():
                            if not first and (known is None or known + 3 < NPAIR):
                                over_low(p.after(3))

                        for t, n in tiles(p, known):
                            if t.u % 2 == 0:
                                chain(t, n, nothing, low_next)
                                if first and (known is None or known + 2 < NPAIR):
                                    over_low(p.after(2))
                            else:
                                chain(t, n, select_ahead, over_low_ahead)
                    run_tiles(dve, NPAIR, PAIRS, body, 3)

                @block.tensor
                def _(pe):
                    if_general(pe, general_tensor)

                    def aggregate(p, known):
                        nodes, edges = (XH[p.u], RH[p.u]) if first else (SelfP[p.u], G[p.u])
                        if first:
                            pe.wait_ge(nodes_made, upto(p))
                            pe.wait_ge(edges_made, upto(p))
                        else:
                            pe.wait_ge(self_in[p.u], 16 * uses(p))
                            pe.wait_ge(edge_in[p.u], 16 * CHUNKS * uses(p))
                        pe.wait_ge(s_made, upto(p))
                        for f in range(KD):
                            fs = slice(f * P, (f + 1) * P)
                            for j in range(2):
                                o = Agg[p.u][:, (2 * f + j) * P:(2 * f + j + 1) * P]
                                nc.tensor.matmul(o, nodes[:, j, fs], ident[:, :], is_transpose=True,
                                                 start=(f % 2 == 0 and j == 0), stop=False, skip_group_check=True)
                                nc.tensor.matmul(o, edges[:, j, fs], S[p.u][:, j, :],
                                                 start=False, stop=False, skip_group_check=True)
                        pe.wait_ge(vlo_done, upto(p))
                        for f in range(KD):
                            for V in (Vhi, Vlo):
                                m = nc.tensor.matmul(Agg[p.u][:, 2 * f * P:2 * (f + 1) * P],
                                                     V[p.u][:, f * P:(f + 1) * P], Sv[p.u][:, :],
                                                     start=False, stop=(V is Vlo), skip_group_check=True)
                        m.then_inc(agg_done, 1)

                    def multiply(p, t, known):
                        pe.wait_ge(hi_done, upto(p))
                        if not third:
                            wait_free(pe, cg_done, t, known)
                        else:
                            if known is not None and known < SLOTS:
                                pe.wait_ge(cg_done, 2 * NT)
                            else:
                                pe.wait_ge(res_done, t.n - SLOTS + 1)
                        n = 0
                        for a, w in ((Ahi, Whi), (Ahi, Wlo), (Alo, Whi)):
                            if a is Alo:
                                pe.wait_ge(lo_done, upto(p))
                            for f in range(KD):
                                c = (2 * f + t.u % 2) * P
                                m = nc.tensor.matmul(Out[t.u][:, :], a[p.u][:, c:c + P], w[q][:, f, :],
                                                     start=(n == 0), stop=(third and n == 3 * KD - 1))
                                n += 1
                        if not third:
                            pe.wait_ge(root_in[p.u], 16 * uses(p))
                            m = nc.tensor.matmul(Out[t.u][:, :], root[p.u][:, t.u % 2, :], B3[q][:, :],
                                                 start=False, stop=True)
                        m.then_inc(main_done, 1)

                    def body(p, known):
                        if known == 0:
                            aggregate(p, 0)
                        if known != NPAIR - 1:
                            aggregate(p.after(1), shifted(known, 1))
                        for t, n in tiles(p, known):
                            multiply(p, t, n)
                    run_tiles(pe, NPAIR, PAIRS, body, 3)

        for q in range(3):
            convolution(q)


_INS = ['x', 'src', 'dst', 'L0_gnn_W1', 'L0_gnn_b1', 'L0_gnn_gamma1', 'L0_gnn_beta1', 'L0_gnn_W2', 'L0_gnn_b2',
        'L0_gnn_gamma2', 'L0_gnn_beta2', 'L1_gnn_W', 'L1_gnn_b']


def kernel(**inputs):
    import numpy as _np
    import concourse.bacc as _bacc
    from concourse import mybir as _mybir
    from concourse.bass_utils import run_bass_kernel_spmd as _run

    nc = _bacc.Bacc("TRN2", target_bir_lowering=False, num_devices=1)
    arrays, args = {}, []
    for name in _INS:
        a = _np.ascontiguousarray(inputs[name])
        arrays[f"in_{name}_dram"] = a
        args.append(nc.dram_tensor(f"in_{name}_dram", a.shape, _mybir.dt.from_np(a.dtype), kind="ExternalInput").ap())
    out = nc.dram_tensor("out_0_dram", inputs["x"].shape, _mybir.dt.float32, kind="ExternalOutput").ap()
    gnn_kernel(nc, *args, out)
    r = _run(nc, [arrays], core_ids=[0])
    return r.results[0]["out_0_dram"]
```
